# Optimizing a Trainium2 kernel written in Bass

```python
import numpy as np
import jax
import jax.numpy as jnp

def _softmax(x, axis=-1):
    return jax.nn.softmax(x, axis=axis)

def _gelu(x):
    return jax.nn.gelu(x, approximate=True)

def _silu(x):
    return jax.nn.silu(x)

def _sigmoid(x):
    return jax.nn.sigmoid(x)

def _layernorm(x, axis=-1, eps=1e-05):
    m = jnp.mean(x, axis=axis, keepdims=True)
    v = jnp.var(x, axis=axis, keepdims=True)
    return (x - m) / jnp.sqrt(v + eps)

def _scatter_add(tgt, idx, src, axis=0):
    return tgt.at[idx].add(src)

def _segment_sum(src, seg, n):
    return jax.ops.segment_sum(src, seg, n)
kernel_name = 'mk_cond_resid_d4_seqx_r8_2746ee'

def setup_inputs(seed: int=0):
    np.random.seed(seed)
    _w = jnp.asarray

    def _rec_inputs():
        import jax
        import jax.numpy as jnp
        _rk = jax.random.key(seed)
        x = 7.22e-05 + 1 * jax.random.normal(jax.random.fold_in(_rk, 1), (8, 128, 512), jnp.float32)
        _lenS = 128 - jax.random.randint(jax.random.fold_in(_rk, 7), (8,), 0, max(1, 128 // 4) + 1, jnp.int32)
        _lenS2 = 128 - jax.random.randint(jax.random.fold_in(_rk, 8), (8,), 0, max(1, 128 // 4) + 1, jnp.int32)
        itok_B_2_6 = jax.random.randint(jax.random.fold_in(_rk, 11), (8,), 2, 7, jnp.int32)
        itok_B_3_7 = jax.random.randint(jax.random.fold_in(_rk, 12), (8,), 3, 8, jnp.int32)
        itok_B_0_2 = jax.random.randint(jax.random.fold_in(_rk, 13), (8,), 0, 3, jnp.int32)
        itok_B_6_15 = jax.random.randint(jax.random.fold_in(_rk, 14), (8,), 6, 16, jnp.int32)
        return (x, itok_B_2_6, itok_B_3_7, itok_B_0_2, itok_B_6_15)
    x, itok_B_2_6, itok_B_3_7, itok_B_0_2, itok_B_6_15 = _rec_inputs()

    def _L0_cond_setup():
        import jax, jax.numpy as jnp
        import numpy as np
        B, N, H, F = (4, 64, 512, 1376)
        L, R, RANK = (1, 16, 16)
        SCALE = 0.5
        key = jax.random.key(seed)
        ks = jax.random.split(key, 12)
        nrm = lambda k, shape, fan: jax.random.normal(k, shape, jnp.float32) * fan ** (-0.5)
        inp = {'x': jax.random.normal(ks[0], (B, N, H), jnp.float32), 'W_gate': nrm(ks[1], (F, H), H), 'W_up': nrm(ks[2], (F, H), H), 'W_down': nrm(ks[3], (H, F), F), 'A_gate': nrm(ks[4], (L, R, RANK, H), H), 'B_gate': nrm(ks[5], (L, R, F, RANK), RANK), 'A_up': nrm(ks[6], (L, R, RANK, H), H), 'B_up': nrm(ks[7], (L, R, F, RANK), RANK), 'A_down': nrm(ks[8], (L, R, RANK, F), F), 'B_down': nrm(ks[9], (L, R, H, RANK), RANK), 'lora_indices': jax.random.randint(ks[10], (B,), 0, R), 'layer_idx': 0}
        return inp
    _L0_cond_all = _L0_cond_setup()
    _L0_cond_in = {k: v for k, v in _L0_cond_all.items() if k in ('W_gate', 'W_up', 'W_down', 'A_gate', 'B_gate', 'A_up', 'B_up', 'A_down', 'B_down')}
    del _L0_cond_all

    def _L1_cond_setup():
        import jax, jax.numpy as jnp
        import numpy as np
        RANK = 16
        ALPHA = 16.0
        SCALING = ALPHA / RANK
        N_ADAPTERS = 8
        IN_F = 512
        OUT_F = 512
        BATCH = 4
        SEQ = 256
        key = jax.random.key(seed)
        kx, ka, kb, ki = jax.random.split(key, 4)
        x = jax.random.normal(kx, (BATCH, SEQ, IN_F), dtype=jnp.float32)
        A = jax.random.normal(ka, (N_ADAPTERS, OUT_F, RANK), dtype=jnp.float32) * 0.02
        B = jax.random.normal(kb, (N_ADAPTERS, RANK, IN_F), dtype=jnp.float32) * 0.02
        adapter_ids = jax.random.randint(ki, (BATCH,), 0, N_ADAPTERS, dtype=jnp.int32)
        return {'x': x, 'A': A, 'B': B, 'adapter_ids': adapter_ids}
    _L1_cond_all = _L1_cond_setup()
    _L1_cond_in = {k: v for k, v in _L1_cond_all.items() if k in ('A', 'B')}
    del _L1_cond_all

    def _L2_cond_setup():
        import jax, jax.numpy as jnp
        import numpy as np
        B, S, D_IN, D_OUT = (4, 256, 512, 512)
        R, NUM_LABELERS = (32, 5)
        LORA_SCALING = 16 / 32
        key = jax.random.key(seed)
        k1, k2, k3, k4, k5 = jax.random.split(key, 5)
        x = jax.random.normal(k1, (B, S, D_IN), dtype=jnp.float32)
        labeler_index = jax.random.randint(k2, (B,), 0, NUM_LABELERS, dtype=jnp.int64)
        W = jax.random.normal(k3, (D_OUT, D_IN), dtype=jnp.float32) * 0.02
        lora_A = jax.random.normal(k4, (NUM_LABELERS, D_IN, R), dtype=jnp.float32) * 0.02
        lora_B_w = jax.random.normal(k5, (D_OUT, R), dtype=jnp.float32) * 0.02
        return {'x': x, 'labeler_index': labeler_index, 'W': W, 'lora_A': lora_A, 'lora_B_w': lora_B_w}
    _L2_cond_all = _L2_cond_setup()
    _L2_cond_in = {k: v for k, v in _L2_cond_all.items() if k in ('W', 'lora_A', 'lora_B_w')}
    del _L2_cond_all

    def _L3_cond_setup():
        import jax, jax.numpy as jnp
        import numpy as np
        B, S, D_IN, D_OUT = (4, 256, 512, 512)
        RANK, MAX_LORAS = (16, 32)
        key = jax.random.key(seed)
        ks = jax.random.split(key, 6)
        x = jax.random.normal(ks[0], (B, S, D_IN), dtype=jnp.float32)
        adapter_ids = jax.random.randint(ks[1], (B,), 0, MAX_LORAS)
        base_weight = jax.random.normal(ks[2], (D_OUT, D_IN), dtype=jnp.float32) * D_IN ** (-0.5)
        base_bias = jax.random.normal(ks[3], (D_OUT,), dtype=jnp.float32) * 0.01
        lora_A_w = jax.random.normal(ks[4], (MAX_LORAS, RANK, D_IN), dtype=jnp.float32) * D_IN ** (-0.5)
        lora_B_w = jax.random.normal(ks[5], (MAX_LORAS, D_OUT, RANK), dtype=jnp.float32) * RANK ** (-0.5)
        return {'x': x, 'adapter_ids': adapter_ids, 'base_weight': base_weight, 'base_bias': base_bias, 'lora_A_w': lora_A_w, 'lora_B_w': lora_B_w}
    _L3_cond_all = _L3_cond_setup()
    _L3_cond_in = {k: v for k, v in _L3_cond_all.items() if k in ('base_weight', 'base_bias', 'lora_A_w', 'lora_B_w')}
    del _L3_cond_all
    return {'x': x, 'itok_B_2_6': itok_B_2_6, 'itok_B_3_7': itok_B_3_7, 'itok_B_0_2': itok_B_0_2, 'itok_B_6_15': itok_B_6_15, 'L0_cond_W_gate': _L0_cond_in['W_gate'], 'L0_cond_W_up': _L0_cond_in['W_up'], 'L0_cond_W_down': _L0_cond_in['W_down'], 'L0_cond_A_gate': _L0_cond_in['A_gate'], 'L0_cond_B_gate': _L0_cond_in['B_gate'], 'L0_cond_A_up': _L0_cond_in['A_up'], 'L0_cond_B_up': _L0_cond_in['B_up'], 'L0_cond_A_down': _L0_cond_in['A_down'], 'L0_cond_B_down': _L0_cond_in['B_down'], 'L1_cond_A': _L1_cond_in['A'], 'L1_cond_B': _L1_cond_in['B'], 'L2_cond_W': _L2_cond_in['W'], 'L2_cond_lora_A': _L2_cond_in['lora_A'], 'L2_cond_lora_B_w': _L2_cond_in['lora_B_w'], 'L3_cond_base_weight': _L3_cond_in['base_weight'], 'L3_cond_base_bias': _L3_cond_in['base_bias'], 'L3_cond_lora_A_w': _L3_cond_in['lora_A_w'], 'L3_cond_lora_B_w': _L3_cond_in['lora_B_w']}

def reference(x, itok_B_2_6, itok_B_3_7, itok_B_0_2, itok_B_6_15, L0_cond_W_gate, L0_cond_W_up, L0_cond_W_down, L0_cond_A_gate, L0_cond_B_gate, L0_cond_A_up, L0_cond_B_up, L0_cond_A_down, L0_cond_B_down, L1_cond_A, L1_cond_B, L2_cond_W, L2_cond_lora_A, L2_cond_lora_B_w, L3_cond_base_weight, L3_cond_base_bias, L3_cond_lora_A_w, L3_cond_lora_B_w):
    import jax
    import jax.numpy as jnp

    def _L0_cond_ref(x, W_gate, W_up, W_down, A_gate, B_gate, A_up, B_up, A_down, B_down, lora_indices, layer_idx):
        import jax, jax.numpy as jnp
        import numpy as np
        B, N, H, F = (4, 64, 512, 1376)
        L, R, RANK = (1, 16, 16)
        SCALE = 0.5

        def lora_add(base, inp, A, B):
            Ab = A[layer_idx][lora_indices]
            Bb = B[layer_idx][lora_indices]
            t = jnp.einsum('bri,bni->bnr', Ab, inp)
            return base + jnp.einsum('bor,bnr->bno', Bb, t) * SCALE
        gate = lora_add(jnp.einsum('bnh,fh->bnf', x, W_gate), x, A_gate, B_gate)
        up = lora_add(jnp.einsum('bnh,fh->bnf', x, W_up), x, A_up, B_up)
        act = jax.nn.silu(gate) * up
        down = lora_add(jnp.einsum('bnf,hf->bnh', act, W_down), act, A_down, B_down)
        return down

    def _L1_cond_ref(x, A, B, adapter_ids):
        import jax, jax.numpy as jnp
        import numpy as np
        RANK = 16
        ALPHA = 16.0
        SCALING = ALPHA / RANK
        N_ADAPTERS = 8
        IN_F = 512
        OUT_F = 512
        BATCH = 4
        SEQ = 256
        B_sel = B[adapter_ids]
        A_sel = A[adapter_ids]
        Bx = jnp.einsum('bni,bri->bnr', x, B_sel)
        out = jnp.einsum('bnr,bor->bno', Bx, A_sel)
        return out * SCALING

    def _L2_cond_ref(x, labeler_index, W, lora_A, lora_B_w):
        import jax, jax.numpy as jnp
        import numpy as np
        B, S, D_IN, D_OUT = (4, 256, 512, 512)
        R, NUM_LABELERS = (32, 5)
        LORA_SCALING = 16 / 32
        base = jnp.einsum('bsi,oi->bso', x, W)
        labelers_A = lora_A[labeler_index]
        low = jnp.einsum('bsi,bir->bsr', x, labelers_A)
        delta = jnp.einsum('bsr,or->bso', low, lora_B_w) * LORA_SCALING
        return base + delta

    def _L3_cond_ref(x, adapter_ids, base_weight, base_bias, lora_A_w, lora_B_w):
        import jax, jax.numpy as jnp
        import numpy as np
        B, S, D_IN, D_OUT = (4, 256, 512, 512)
        RANK, MAX_LORAS = (16, 32)
        result = jnp.einsum('bsd,od->bso', x, base_weight) + base_bias
        A = lora_A_w[adapter_ids]
        Bw = lora_B_w[adapter_ids]
        h = jnp.einsum('bsd,brd->bsr', x, A)
        lora_out = jnp.einsum('bsr,bor->bso', h, Bw)
        result = result + lora_out
        return result.astype(x.dtype)
    x = x + _L0_cond_ref(x, L0_cond_W_gate, L0_cond_W_up, L0_cond_W_down, L0_cond_A_gate, L0_cond_B_gate, L0_cond_A_up, L0_cond_B_up, L0_cond_A_down, L0_cond_B_down, itok_B_2_6, 0)
    x = x + _L1_cond_ref(x, L1_cond_A, L1_cond_B, itok_B_3_7)
    x = x + _L2_cond_ref(x, itok_B_0_2, L2_cond_W, L2_cond_lora_A, L2_cond_lora_B_w)
    x = x + _L3_cond_ref(x, itok_B_6_15, L3_cond_base_weight, L3_cond_base_bias, L3_cond_lora_A_w, L3_cond_lora_B_w)
    return x

_drawn_inputs = setup_inputs


def setup_inputs(seed=0):
    import zlib

    import numpy as np

    out = dict(_drawn_inputs(seed))
    spreads = {}
    factors = {'L2_cond_lora_A': 2.713, 'L2_cond_lora_B_w': 2.72, 'L3_cond_base_bias': 8.0}
    for name, (base, spread) in spreads.items():
        noise = np.random.default_rng([zlib.crc32(name.encode()), seed]).standard_normal(out[name].shape)
        drawn = base * np.exp(spread * noise) if base else spread * noise
        out[name] = jnp.asarray(drawn.astype(out[name].dtype))
    for name, factor in factors.items():
        out[name] = (out[name] * factor).astype(out[name].dtype)
    return out
```

```python
from contextlib import ExitStack

import concourse.bass as bass
from concourse import mybir

F32 = mybir.dt.float32
F32R = mybir.dt.float32r
ALU = mybir.AluOpType
ACT = mybir.ActivationFunctionType
DVE_ENGINE = mybir.EngineType.DVE
ACT_ENGINE = mybir.EngineType.Activation
PE_ENGINE = mybir.EngineType.PE
SP_ENGINE = mybir.EngineType.SP
POOL_ENGINE = mybir.EngineType.Pool

P = 128
BATCH, SEQ, HID, FFN = 8, 128, 512, 1376
TOK = BATCH * SEQ
KT = HID // P
FT = -(-FFN // P)
FPAD = FT * P
HALF = TOK // 2
PAIRS = BATCH // 2
PT = 2 * SEQ
RANK = 16
COPIES = 4
DOWN_TILES = KT * FT
PER_CHUNK = 8
CHUNK = PER_CHUNK * P
DOWN_CHUNKS = -(-DOWN_TILES // PER_CHUNK)
CHUNKS = FT + DOWN_CHUNKS
B_BLOCKS = FT + KT // 2
L0_SCALE, L2_SCALE = 0.5, 0.5
ADAPTERS = {"l0": 16, "l1": 8, "l2": 5, "l3": 32}


def lora_chain_kernel(nc, x_t, weights, indices, gu_a, up_b, down_a, l1_b, l1_a, l2_w, l2_a, l2_b,
                      l3_w, l3_a, l3_b, bias, row_signs, out):
    ctx = ExitStack()
    with ctx:
        def sb(name, shape, dt=F32):
            return ctx.enter_context(nc.sbuf_tensor(name, shape, dt))

        def sem(name):
            return ctx.enter_context(nc.semaphore(name))

        act_hl = sb("act_hl", [P, FT, 2, TOK], F32R)
        x_hl = sb("x_hl", [P, 2, KT, TOK], F32R)
        w_hl = sb("w_hl", [P, 2, 2, CHUNK], F32R)
        b_rows = sb("b_rows", [P, 2, PAIRS, 2 * P], F32R)
        down_a_cols = sb("down_a_cols", [P, 2, PAIRS, P], F32R)
        t_rows = sb("t_rows", [P, 2 * PAIRS * PT], F32R)
        zeros = sb("zeros", [P, PT], F32R)

        def act_space(tile, n):
            return act_hl[:, tile:tile + n, :, :].rearrange("p a b c -> p (a b c)")

        gu_a_cols = act_space(9, 2).rearrange("p (w k c) -> p w k c", w=2, k=KT)
        l2_w_hl = act_space(0, 2).rearrange("p (s k o) -> p s k o", s=2, k=KT)
        l1_b_cols = act_space(2, 1).rearrange("p (k c) -> p k c", k=KT)
        l1_a_rows = act_space(3, 1).rearrange("p (r o) -> p r o", r=PAIRS)
        l2_a_cols = act_space(4, 2).rearrange("p (k r v c) -> p k r v c", k=KT, r=PAIRS, v=2)
        l2_b_rows = act_space(6, 1)[:, 0:HID]
        l3_b_rows = l1_a_rows
        x3_hl = act_space(7, 4).rearrange("p (s k t) -> p s k t", s=2, k=KT)
        l3_w_hl = w_hl[:, :, :, :].rearrange("p a b c -> p (a b c)").rearrange(
            "p (s k o) -> p s k o", s=2, k=KT)
        l3_a_cols = b_rows[:, :, :, :].rearrange("p a b c -> p (a b c)").rearrange(
            "p (k c) -> p k c", k=KT)

        x_res = sb("x_res", [P, KT, TOK])
        w_raw = sb("w_raw", [P, 2, CHUNK])
        b_raw = sb("b_raw", [P, PAIRS, 2 * P])
        down_a_raw = sb("down_a_raw", [P, BATCH, FT, RANK])
        low_raw = sb("low_raw", [P, 4 * HID])
        silu_out = sb("silu_out", [P, 4 * HID])
        bias_col = sb("bias_col", [P, KT])
        sign_col = sb("sign_col", [P, 2])
        t_sign, b_sign = sign_col[:, 0:1], sign_col[:, 1:2]
        t_sign_half = sb("t_sign_half", [P, 1])

        down_a_flat = down_a_raw[:, :, :, :].rearrange("p a b c -> p (a b c)")
        gu_a_raw = low_raw[:, 0:1024].rearrange("p (b w k r) -> p b w k r", b=BATCH, w=2, k=KT)
        l1_b_raw = down_a_flat[:, 0:512].rearrange("p (b k r) -> p b k r", b=BATCH, k=KT)
        l2_b_raw = down_a_flat[:, 512:1024]
        l1_a_raw = low_raw[:, :].rearrange("p (r o) -> p r o", r=PAIRS)
        l2_w_raw = silu_out[:, :].rearrange("p (k o) -> p k o", k=KT)
        l2_a_raw = b_raw[:, :, :].rearrange("p a b -> p (a b)").rearrange(
            "p (k b c) -> p k b c", k=KT, b=BATCH)
        l3_w_raw = w_raw[:, :, :].rearrange("p a b -> p (a b)").rearrange("p (k o) -> p k o", k=KT)
        l3_a_raw = l1_b_raw
        l3_b_raw = l1_a_raw

        banks = ctx.enter_context(nc.psum_tensor("banks", [P, 8, 512], F32))

        piece_landed = [sem(f"piece_landed{c}") for c in range(2 * KT)]
        consts_landed = sem("consts_landed")
        piece_hi = sem("piece_hi")
        piece_ready = sem("piece_ready")
        w_landed = [sem(f"w_landed{s}") for s in range(2)]
        w_hi = sem("w_hi")
        w_ready = sem("w_ready")
        b_landed = sem("b_landed")
        b_signed = sem("b_signed")
        b_ready = sem("b_ready")
        gu_a_landed = sem("gu_a_landed")
        gu_a_hi = sem("gu_a_hi")
        gu_a_ready = sem("gu_a_ready")
        down_a_landed = sem("down_a_landed")
        down_a_hi = sem("down_a_hi")
        down_a_ready = sem("down_a_ready")
        t_zeroed = sem("t_zeroed")
        sign_scaled = sem("sign_scaled")
        low_done = sem("low_done")
        t_signed = sem("t_signed")
        t_ready = sem("t_ready")
        gate_up_done = sem("gate_up_done")
        silu_done = sem("silu_done")
        product_done = sem("product_done")
        act_hi = sem("act_hi")
        act_ready = sem("act_ready")
        down_chunk_used = sem("down_chunk_used")
        act_tile_used = sem("act_tile_used")
        group_done = sem("group_done")
        x_summed = sem("x_summed")
        x_hi = sem("x_hi")
        x_ready = sem("x_ready")
        late_landed = {n: sem(f"{n}_landed") for n in
                       ("l2_w", "l1_b", "l1_a", "l2_a", "l2_b", "l3_w", "l3_a", "l3_b")}
        late_hi = sem("late_hi")
        late_ready = sem("late_ready")
        out_stored = sem("out_stored")
        LATE = {n: i + 1 for i, n in enumerate(
            ("l2_w", "l1_b", "l1_a", "l2_a", "l2_b", "l3_w", "l3_a", "l3_b"))}
        GROUPS = 2 * KT
        DOWN0, L1_0, L2_0, L3_0 = 0, GROUPS, 2 * GROUPS, 3 * GROUPS

        def half_of(h):
            return slice(h * HALF, (h + 1) * HALF)

        def pair_of(pair):
            return slice(pair * PT, (pair + 1) * PT)

        def cols_view(cols):
            v = cols.rearrange("p (b r g) -> p b r g", r=RANK, g=COPIES)
            return v[:, :, :, 0:3], v[:, :, :, 3]

        def group_id(base, ht, h):
            return base + (2 * ht + h if base == DOWN0 else KT * h + ht)

        block = ctx.enter_context(nc.Block())

        @block.sync
        def _(sp):
            for c in range(2 * KT):
                h, k = divmod(c, KT)
                if h == 0:
                    sp.dma_start(w_raw[:, 0, k * 256:(k + 1) * 256],
                                 weights[0, :, k * 256:(k + 1) * 256]).then_inc(piece_landed[c], 16)
                sp.dma_start(x_res[:, k, half_of(h)], x_t[k, :, half_of(h)]).then_inc(piece_landed[c], 16)
                if c == 0:
                    sp.dma_start(sign_col[:, :], row_signs).then_inc(consts_landed, 16)
            sp.dma_start(bias_col[:, :], bias).then_inc(consts_landed, 16)
            sp.dma_start(w_raw[:, 1, :], weights[1]).then_inc(w_landed[1], 16)
            sp.wait_ge(piece_ready, KT)
            sp.dma_start(w_raw[:, 0, :], weights[2]).then_inc(w_landed[0], 16)
            with nc.Fori(0, (CHUNKS - 3) // 2, engines=[SP_ENGINE]) as i:
                for u in range(2):
                    sp.wait_ge(w_ready, 2 * i + (1 + u))
                    sp.dma_start(w_raw[:, (1 + u) % 2, :], weights[bass.ds(2 * i + (3 + u), 1)].rearrange(
                        "a p c -> (a p) c")).then_inc(w_landed[(1 + u) % 2], 16)
            sp.wait_ge(act_ready, 2 * FT)
            sp.dma_start(silu_out[:, :], l2_w).then_inc(late_landed["l2_w"], 16)
            sp.wait_ge(down_a_ready, FT)
            sp.dma_start(l2_b_raw, l2_b).then_inc(late_landed["l2_b"], 16)
            sp.wait_ge(w_ready, CHUNKS - 1)
            sp.dma_start(w_raw[:, :, :].rearrange("p a b -> p (a b)"), l3_w).then_inc(
                late_landed["l3_w"], 16)
            for h in range(2):
                for ht in range(KT):
                    sp.wait_ge(x_summed, group_id(L3_0, ht, h) + 1)
                    sp.dma_start(out[ht, :, half_of(h)], x_res[:, ht, half_of(h)]).then_inc(out_stored, 16)
            sp.wait_ge(out_stored, 16 * GROUPS)

        @block.gpsimd
        def _(pool):
            def adapters(layer, name):
                at = layer * BATCH
                return [pool.value_load(indices[0:1, at + b:at + b + 1], min_val=0,
                                        max_val=ADAPTERS[name] - 1) for b in range(BATCH)]

            def gather_cols(table, adapter, raw_of, landed):
                for b in range(BATCH):
                    src = table[bass.ds(adapter[b], 1)]
                    src = src.rearrange("a p k r -> (a p) k r") if len(src.shape) == 4 else \
                        src.rearrange("a p c -> (a p) c")
                    pool.dma_start(raw_of(b), src).then_inc(landed, 16)

            def gather_rows(table, adapter, raw, landed):
                for b in range(BATCH):
                    src = table(adapter[b])
                    n = src.shape[-1]
                    rows = slice(64 * (b % 2), 64 * (b % 2) + 64)
                    pool.dma_start(raw[rows, b // 2, :], src.unsqueeze(1).broadcast_to(
                        [RANK, COPIES, n])).then_inc(landed, 16)

            nc.gpsimd.memset(zeros[:, :].bitcast(F32), 0.0)
            nc.gpsimd.memset(t_rows[:, :].bitcast(F32), 0.0).then_inc(t_zeroed, 1)
            l0 = adapters(0, "l0")
            gather_cols(gu_a, l0, lambda b: gu_a_raw[:, b, :, :, :].rearrange(
                "p w k r -> p (w k r)"), gu_a_landed)

            def b_block(n):
                return lambda a: up_b[bass.ds(a, 1), n].rearrange("a r c -> (a r) c")

            gather_rows(b_block(0), l0, b_raw, b_landed)
            gather_cols(down_a, l0, lambda b: down_a_raw[:, b, :, :].rearrange(
                "p f r -> p (f r)"), down_a_landed)
            with nc.Fori(1, B_BLOCKS, engines=[POOL_ENGINE]) as n:
                pool.wait_ge(b_ready, n)
                gather_rows(lambda a: up_b[bass.ds(a, 1), bass.ds(n, 1)].rearrange(
                    "a n r c -> (a n r) c"), l0, b_raw, b_landed)
            l1 = adapters(1, "l1")
            pool.wait_ge(down_a_ready, FT)
            gather_cols(l1_b, l1, lambda b: l1_b_raw[:, b, :, :].rearrange("p k r -> p (k r)"),
                        late_landed["l1_b"])
            pool.wait_ge(gu_a_ready, 1)
            gather_rows(lambda a: l1_a[bass.ds(a, 1)].rearrange("a r o -> (a r) o"), l1, l1_a_raw,
                        late_landed["l1_a"])
            l2 = adapters(2, "l2")
            pool.wait_ge(b_ready, B_BLOCKS)
            gather_cols(l2_a, l2, lambda b: l2_a_raw[:, :, b, :], late_landed["l2_a"])
            l3 = adapters(3, "l3")
            pool.wait_ge(late_ready, LATE["l1_b"])
            gather_cols(l3_a, l3, lambda b: l3_a_raw[:, b, :, :].rearrange("p k r -> p (k r)"),
                        late_landed["l3_a"])
            pool.wait_ge(late_ready, LATE["l1_a"])
            gather_rows(lambda a: l3_b[bass.ds(a, 1)].rearrange("a r o -> (a r) o"), l3, l3_b_raw,
                        late_landed["l3_b"])

        @block.scalar
        def _(act):
            def hi(dst, src):
                return nc.scalar.activation(dst, src, ACT.Copy)

            def signed(dst, src, sign):
                return nc.scalar.activation(dst, src, ACT.Copy, scale=sign)

            for c in range(2 * KT):
                h, k = divmod(c, KT)
                act.wait_ge(piece_landed[c], 32 if h == 0 else 16)
                if h == 0:
                    hi(w_hl[:, 0, 0, k * 256:(k + 1) * 256], w_raw[:, 0, k * 256:(k + 1) * 256])
                hi(x_hl[:, 0, k, half_of(h)], x_res[:, k, half_of(h)]).then_inc(piece_hi, 1)
            act.wait_ge(gu_a_landed, 16 * BATCH)
            for w in range(2):
                for k in range(KT):
                    his, _ = cols_view(gu_a_cols[:, w, k, :])
                    last = hi(his, gu_a_raw[:, :, w, k, :].unsqueeze(3).broadcast_to([P, BATCH, RANK, 3]))
            last.then_inc(gu_a_hi, 1)
            act.wait_ge(consts_landed, 32)
            act.wait_ge(sign_scaled, 1)

            def b_block_signed(n, slot, landed):
                act.wait_ge(b_landed, landed)
                signed(b_rows[:, slot, :, :], b_raw[:, :, :], b_sign).then_inc(b_signed, 1)

            def down_a_split(ft, slot):
                his, _ = cols_view(down_a_cols[:, slot, :, :].rearrange("p a c -> p (a c)"))
                hi(his, down_a_raw[:, :, ft, :].unsqueeze(3).broadcast_to(
                    [P, BATCH, RANK, 3])).then_inc(down_a_hi, 1)

            def t_split(event, row_half, dst, src, sign):
                rows = slice(64 * row_half, 64 * row_half + 64)
                return signed(dst[rows], src[rows], sign[rows])

            def ffn_half(ft, h, step, first):
                act.wait_ge(gate_up_done, step + 1)
                if not first:
                    act.wait_ge(act_ready, step - 1)
                nc.scalar.activation(silu_out[:, half_of(h)], banks[:, 2 * h, :], ACT.Silu).then_inc(
                    silu_done, 1)

            def ffn_hi(ft, h, step):
                act.wait_ge(product_done, step + 1)
                hi(act_hl[:, ft, 0, half_of(h)], silu_out[:, half_of(h)]).then_inc(act_hi, 1)

            def weights_hi(slot, landed):
                act.wait_ge(w_landed[slot], landed)
                hi(w_hl[:, slot, 0, :], w_raw[:, slot, :]).then_inc(w_hi, 1)

            b_block_signed(0, 0, 16 * BATCH)
            act.wait_ge(low_done, 1)
            act.wait_ge(t_zeroed, 1)
            gu_low = banks[:, 4:8, :].rearrange("p a (w t) -> p (a w) t", w=2)
            gu_t = t_rows[:, :].rearrange("p (a t) -> p a t", t=PT)
            for r in range(2):
                last = t_split(1, r, gu_t[:, :, r * SEQ:(r + 1) * SEQ], gu_low[:, :, r * SEQ:(r + 1) * SEQ],
                               t_sign_half)
            last.then_inc(t_signed, 1)
            weights_hi(1, 16)
            act.wait_ge(down_a_landed, 16 * BATCH)
            ffn_half(0, 0, 0, True)
            ffn_hi(0, 0, 0)
            ffn_half(0, 1, 1, True)
            b_block_signed(1, 1, 2 * 16 * BATCH)
            down_a_split(0, 0)
            ffn_hi(0, 1, 1)
            with nc.Fori(0, (FT - 1) // 2, engines=[ACT_ENGINE]) as i:
                for u in range(2):
                    ft, slot = 2 * i + (1 + u), (1 + u) % 2
                    ft_at = bass.ds(ft, 1)

                    def act_at(h):
                        return act_hl[:, ft_at, 0, half_of(h)].rearrange("p a t -> p (a t)")

                    for h in range(2):
                        step = 4 * i + (2 + 2 * u + h)
                        act.wait_ge(gate_up_done, step + 1)
                        act.wait_ge(act_ready, step - 1)
                        nc.scalar.activation(silu_out[:, half_of(h)], banks[:, 2 * h, :],
                                             ACT.Silu).then_inc(silu_done, 1)
                        if h == 0:
                            act.wait_ge(w_landed[1 - slot], 16 * i + 16 * (1 + u))
                            hi(w_hl[:, 1 - slot, 0, :], w_raw[:, 1 - slot, :]).then_inc(w_hi, 1)
                        else:
                            act.wait_ge(b_landed, 256 * i + 16 * BATCH * (3 + u))
                            signed(b_rows[:, 1 - slot, :, :], b_raw[:, :, :], b_sign).then_inc(b_signed, 1)
                            his, _ = cols_view(down_a_cols[:, slot, :, :].rearrange("p a c -> p (a c)"))
                            hi(his, down_a_raw[:, :, ft_at, :].rearrange("p b f r -> p b (f r)").unsqueeze(
                                3).broadcast_to([P, BATCH, RANK, 3])).then_inc(down_a_hi, 1)
                        act.wait_ge(product_done, step + 1)
                        hi(act_at(h), silu_out[:, half_of(h)]).then_inc(act_hi, 1)
            b_block_signed(B_BLOCKS - 1, 0, 16 * BATCH * B_BLOCKS)
            weights_hi(0, 16 * (FT + 1) // 2)
            act.wait_ge(low_done, 2)
            down_t = t_rows[:, 0:PAIRS * PT].rearrange("p (a t) -> p a t", t=PT)
            for r in range(2):
                at = slice(r * SEQ, (r + 1) * SEQ)
                last = t_split(2, r, down_t[:, :, at], banks[:, 4:8, at], t_sign_half)
            last.then_inc(t_signed, 1)

            def down_chunk_hi(c):
                act.wait_ge(down_chunk_used, c - 1)
                n = FT + c
                slot = n % 2
                act.wait_ge(w_landed[slot], 16 * ((n + 1) // 2))
                m = min(PER_CHUNK, DOWN_TILES - c * PER_CHUNK) * P
                hi(w_hl[:, slot, 0, 0:m], w_raw[:, slot, 0:m]).then_inc(w_hi, 1)

            def x_hi_part(base, ht, h):
                act.wait_ge(x_summed, group_id(base, ht, h) + 1)
                dst = x3_hl if base == L2_0 else x_hl
                hi(dst[:, 0, ht, half_of(h)], x_res[:, ht, half_of(h)]).then_inc(x_hi, 1)

            def cols_hi(name, cols, raw):
                act.wait_ge(late_landed[name], 16 * BATCH)
                for k in range(KT):
                    his, _ = cols_view(cols[:, k, :])
                    last = hi(his, raw[:, :, k, :].unsqueeze(3).broadcast_to([P, BATCH, RANK, 3]))
                last.then_inc(late_hi, 1)

            def rows_signed(name, rows, raw, gathers):
                act.wait_ge(late_landed[name], 16 * gathers)
                signed(rows, raw, b_sign).then_inc(late_hi, 1)

            def matrix_hi(name, dst, raw):
                act.wait_ge(late_landed[name], 16)
                hi(dst[:, 0, :, :], raw).then_inc(late_hi, 1)

            def low_signed(event, pairs, bank_cols, base, sign):
                act.wait_ge(low_done, event)
                for r in range(2):
                    at = slice(r * SEQ, (r + 1) * SEQ)
                    dst = t_rows[:, base:base + PAIRS * PT].rearrange("p (a t) -> p a t", t=PT)
                    last = t_split(event, r, dst[:, pairs, at], banks[:, 4 + pairs.start:4 + pairs.stop, at],
                                   sign)
                last.then_inc(t_signed, 1)

            down_chunk_hi(2)
            for h in range(2):
                x_hi_part(DOWN0, 0, h)
            down_chunk_hi(3)
            for h in range(2):
                x_hi_part(DOWN0, 1, h)
            down_chunk_hi(4)
            down_chunk_hi(5)
            for h in range(2):
                x_hi_part(DOWN0, 2, h)
            act.wait_ge(act_tile_used, 2)
            matrix_hi("l2_w", l2_w_hl, l2_w_raw)
            act.wait_ge(act_tile_used, 3)
            cols_hi("l1_b", l1_b_cols, l1_b_raw)
            act.wait_ge(act_tile_used, 4)
            rows_signed("l1_a", l1_a_rows, l1_a_raw, BATCH)
            act.wait_ge(act_tile_used, 6)
            act.wait_ge(late_landed["l2_a"], 16 * BATCH)
            for blk in range(2):
                for q in range(2):
                    v = l2_a_cols[:, :, :, blk ^ q, 64 * q:64 * q + 64].rearrange(
                        "p k a (r g) -> p (k a) r g", g=COPIES)
                    raw = l2_a_raw[:, :, :, RANK * q:RANK * q + RANK].rearrange(
                        "p k (a two) r -> p (k a) two r", two=2)[:, :, blk, :]
                    last = hi(v[:, :, :, 0:3], raw.unsqueeze(3).broadcast_to([P, KT * PAIRS, RANK, 3]))
            last.then_inc(late_hi, 1)
            act.wait_ge(act_tile_used, 7)
            rows_signed("l2_b", l2_b_rows, l2_b_raw, 1)
            for h in range(2):
                x_hi_part(DOWN0, 3, h)
            for h in range(2):
                low_signed(3 + h, slice(2 * h, 2 * h + 2), None, PAIRS * PT, t_sign)
            for h in range(2):
                for ht in range(KT):
                    x_hi_part(L1_0, ht, h)
            def l2_low_signed(h):
                act.wait_ge(low_done, 5 + h)
                for pair in range(2 * h, 2 * h + 2):
                    for blk in range(2):
                        for q in range(2):
                            rows = slice(64 * q, 64 * q + 64)
                            c0 = PT * (blk ^ q) + SEQ * blk
                            last = signed(t_rows[rows, pair * PT + blk * SEQ:pair * PT + blk * SEQ + SEQ],
                                          banks[rows, 4 + pair, c0:c0 + SEQ], t_sign_half[rows])
                last.then_inc(t_signed, 1)

            l2_low_signed(0)
            matrix_hi("l3_w", l3_w_hl, l3_w_raw)
            cols_hi("l3_a", l3_a_cols, l3_a_raw)
            x_hi_part(L2_0, 0, 0)
            rows_signed("l3_b", l3_b_rows, l3_b_raw, BATCH)
            for ht in range(1, KT):
                x_hi_part(L2_0, ht, 0)
            l2_low_signed(1)
            for ht in range(KT):
                x_hi_part(L2_0, ht, 1)
            for h in range(2):
                low_signed(7 + h, slice(2 * h, 2 * h + 2), None, PAIRS * PT, t_sign)

        @block.vector
        def _(dve):
            def lo(dst, src, hi_part):
                return nc.vector.tensor_tensor(dst, src, hi_part.bitcast(F32), ALU.subtract)

            def add_signed(rows, raw):
                return nc.vector.tensor_tensor(rows, raw, rows.bitcast(F32), ALU.add)

            dve.wait_ge(consts_landed, 32)
            nc.vector.tensor_scalar(t_sign_half[:, :], t_sign, L0_SCALE, None, ALU.mult).then_inc(
                sign_scaled, 1)
            for c in range(2 * KT):
                h, k = divmod(c, KT)
                dve.wait_ge(piece_hi, c + 1)
                if h == 0:
                    at = slice(k * 256, (k + 1) * 256)
                    lo(w_hl[:, 0, 1, at], w_raw[:, 0, at], w_hl[:, 0, 0, at])
                lo(x_hl[:, 1, k, half_of(h)], x_res[:, k, half_of(h)], x_hl[:, 0, k, half_of(h)]).then_inc(
                    piece_ready, 1)

            def cols_lo(cols, raw):
                his, los = cols_view(cols)
                return lo(los, raw, his[:, :, :, 0])

            dve.wait_ge(gu_a_hi, 1)
            for w in range(2):
                for k in range(KT):
                    last = cols_lo(gu_a_cols[:, w, k, :], gu_a_raw[:, :, w, k, :])
            last.then_inc(gu_a_ready, 1)

            def b_block_add(n, slot):
                dve.wait_ge(b_signed, n + 1)
                add_signed(b_rows[:, slot, :, :], b_raw[:, :, :]).then_inc(b_ready, 1)

            def t_add(rows, dst, src, scale):
                return nc.vector.scalar_tensor_tensor(out=dst[rows], in0=src[rows], scalar=scale,
                                                      in1=dst[rows].bitcast(F32), op0=ALU.mult,
                                                      op1=ALU.add)

            b_block_add(0, 0)
            dve.wait_ge(t_signed, 1)
            gu_low = banks[:, 4:8, :].rearrange("p a (w t) -> p (a w) t", w=2)
            gu_t = t_rows[:, :].rearrange("p (a t) -> p a t", t=PT)
            for r in range(2):
                at = slice(r * SEQ, (r + 1) * SEQ)
                last = t_add(slice(64 * r, 64 * r + 64), gu_t[:, :, at], gu_low[:, :, at], L0_SCALE)
            last.then_inc(t_ready, 1)

            def weights_lo(slot, count, m=CHUNK):
                dve.wait_ge(w_hi, count)
                lo(w_hl[:, slot, 1, 0:m], w_raw[:, slot, 0:m], w_hl[:, slot, 0, 0:m]).then_inc(w_ready, 1)

            def product(h, step):
                dve.wait_ge(silu_done, step + 1)
                nc.vector.tensor_tensor(silu_out[:, half_of(h)], banks[:, 2 * h + 1, :],
                                        silu_out[:, half_of(h)], ALU.mult).then_inc(product_done, 1)

            weights_lo(1, 1)
            for h in range(2):
                product(h, h)
                if h == 1:
                    b_block_add(1, 1)
                    dve.wait_ge(down_a_hi, 1)
                    cols_lo(down_a_cols[:, 0, :, :].rearrange("p a c -> p (a c)"),
                            down_a_raw[:, :, 0, :]).then_inc(down_a_ready, 1)
                dve.wait_ge(act_hi, h + 1)
                lo(act_hl[:, 0, 1, half_of(h)], silu_out[:, half_of(h)],
                   act_hl[:, 0, 0, half_of(h)]).then_inc(act_ready, 1)
            with nc.Fori(0, (FT - 1) // 2, engines=[DVE_ENGINE]) as i:
                for u in range(2):
                    ft, slot = 2 * i + (1 + u), (1 + u) % 2
                    ft_at = bass.ds(ft, 1)
                    for h in range(2):
                        step = 4 * i + (2 + 2 * u + h)
                        dve.wait_ge(silu_done, step + 1)
                        nc.vector.tensor_tensor(silu_out[:, half_of(h)], banks[:, 2 * h + 1, :],
                                                silu_out[:, half_of(h)], ALU.mult).then_inc(
                                                    product_done, 1)
                        if h == 0:
                            dve.wait_ge(w_hi, ft + 1)
                            lo(w_hl[:, 1 - slot, 1, :], w_raw[:, 1 - slot, :],
                               w_hl[:, 1 - slot, 0, :]).then_inc(w_ready, 1)
                        else:
                            dve.wait_ge(b_signed, ft + 2)
                            add_signed(b_rows[:, 1 - slot, :, :], b_raw[:, :, :]).then_inc(b_ready, 1)
                            dve.wait_ge(down_a_hi, ft + 1)
                            cols_lo(down_a_cols[:, slot, :, :].rearrange("p a c -> p (a c)"),
                                    down_a_raw[:, :, ft_at, :].rearrange(
                                        "p b f r -> p b (f r)")).then_inc(down_a_ready, 1)
                        dve.wait_ge(act_hi, step + 1)
                        lo(act_hl[:, ft_at, 1, half_of(h)].rearrange("p a t -> p (a t)"),
                           silu_out[:, half_of(h)],
                           act_hl[:, ft_at, 0, half_of(h)].rearrange("p a t -> p (a t)")).then_inc(
                               act_ready, 1)
            b_block_add(B_BLOCKS - 1, 0)
            weights_lo(0, FT + 1)
            dve.wait_ge(t_signed, 2)
            down_t = t_rows[:, 0:PAIRS * PT].rearrange("p (a t) -> p a t", t=PT)
            for r in range(2):
                at = slice(r * SEQ, (r + 1) * SEQ)
                last = t_add(slice(64 * r, 64 * r + 64), down_t[:, :, at], banks[:, 4:8, at], L0_SCALE)
            last.then_inc(t_ready, 1)

            def down_chunk_lo(c):
                weights_lo((FT + c) % 2, FT + c, min(PER_CHUNK, DOWN_TILES - c * PER_CHUNK) * P)

            def x_sum(base, ht, h):
                g = group_id(base, ht, h)
                dve.wait_ge(group_done, g + 1)
                nc.vector.tensor_tensor(x_res[:, ht, half_of(h)], banks[:, g % 4, :],
                                        x_res[:, ht, half_of(h)], ALU.add).then_inc(x_summed, 1)

            def x_lo_part(base, ht, h):
                dve.wait_ge(x_hi, group_id(base, ht, h) + 1)
                dst = x3_hl if base == L2_0 else x_hl
                lo(dst[:, 1, ht, half_of(h)], x_res[:, ht, half_of(h)],
                   dst[:, 0, ht, half_of(h)]).then_inc(x_ready, 1)

            def late(name):
                dve.wait_ge(late_hi, LATE[name])

            def x_groups(base, which):
                for i, (ht, h) in enumerate(which):
                    x_sum(base, ht, h)
                    if i:
                        x_lo_part(base, *which[i - 1])
                x_lo_part(base, *which[-1])

            down_chunk_lo(2)
            x_groups(DOWN0, [(0, 0), (0, 1)])
            down_chunk_lo(3)
            x_groups(DOWN0, [(1, 0), (1, 1)])
            down_chunk_lo(4)
            down_chunk_lo(5)
            x_groups(DOWN0, [(2, 0), (2, 1)])
            late("l2_w")
            lo(l2_w_hl[:, 1, :, :], l2_w_raw, l2_w_hl[:, 0, :, :]).then_inc(late_ready, 1)
            late("l1_b")
            for k in range(KT):
                last = cols_lo(l1_b_cols[:, k, :], l1_b_raw[:, :, k, :])
            last.then_inc(late_ready, 1)
            late("l1_a")
            add_signed(l1_a_rows, l1_a_raw).then_inc(late_ready, 1)
            late("l2_a")
            for blk in range(2):
                for q in range(2):
                    v = l2_a_cols[:, :, :, blk ^ q, 64 * q:64 * q + 64].rearrange(
                        "p k a (r g) -> p (k a) r g", g=COPIES)
                    raw = l2_a_raw[:, :, :, RANK * q:RANK * q + RANK].rearrange(
                        "p k (a two) r -> p (k a) two r", two=2)[:, :, blk, :]
                    last = lo(v[:, :, :, 3], raw, v[:, :, :, 0])
            last.then_inc(late_ready, 1)
            late("l2_b")
            add_signed(l2_b_rows, l2_b_raw).then_inc(late_ready, 1)
            x_groups(DOWN0, [(3, 0), (3, 1)])

            def low_add(event, pairs, scale):
                dve.wait_ge(t_signed, event)
                dst = t_rows[:, PAIRS * PT:2 * PAIRS * PT].rearrange("p (a t) -> p a t", t=PT)
                for r in range(2):
                    at = slice(r * SEQ, (r + 1) * SEQ)
                    last = t_add(slice(64 * r, 64 * r + 64), dst[:, pairs, at],
                                 banks[:, 4 + pairs.start:4 + pairs.stop, at], scale)
                last.then_inc(t_ready, 1)

            def l2_low_add(h):
                dve.wait_ge(t_signed, 5 + h)
                for pair in range(2 * h, 2 * h + 2):
                    for blk in range(2):
                        for q in range(2):
                            c0 = PT * (blk ^ q) + SEQ * blk
                            last = t_add(slice(64 * q, 64 * q + 64),
                                         t_rows[:, pair * PT + blk * SEQ:pair * PT + blk * SEQ + SEQ],
                                         banks[:, 4 + pair, c0:c0 + SEQ], L2_SCALE)
                last.then_inc(t_ready, 1)

            for h in range(2):
                low_add(3 + h, slice(2 * h, 2 * h + 2), 1.0)
            x_groups(L1_0, [(ht, h) for h in range(2) for ht in range(KT)])
            l2_low_add(0)
            late("l3_w")
            dve.wait_ge(group_done, DOWN0 + GROUPS)
            lo(l3_w_hl[:, 1, :, :], l3_w_raw, l3_w_hl[:, 0, :, :]).then_inc(late_ready, 1)
            late("l3_a")
            for k in range(KT):
                last = cols_lo(l3_a_cols[:, k, :], l3_a_raw[:, :, k, :])
            last.then_inc(late_ready, 1)
            x_groups(L2_0, [(0, 0)])
            late("l3_b")
            add_signed(l3_b_rows, l3_b_raw).then_inc(late_ready, 1)
            x_groups(L2_0, [(ht, 0) for ht in range(1, KT)])
            l2_low_add(1)
            x_groups(L2_0, [(ht, 1) for ht in range(KT)])
            for h in range(2):
                low_add(7 + h, slice(2 * h, 2 * h + 2), 1.0)
                for ht in range(KT):
                    g = group_id(L3_0, ht, h)
                    dve.wait_ge(group_done, g + 1)
                    nc.vector.scalar_tensor_tensor(
                        out=x_res[:, ht, half_of(h)], in0=banks[:, g % 4, :],
                        scalar=bias_col[:, ht:ht + 1], in1=x_res[:, ht, half_of(h)],
                        op0=ALU.add, op1=ALU.add).then_inc(x_summed, 1)

        @block.tensor
        def _(pe):
            def passes(dst, w_hi_tile, w_lo_tile, m_hi, m_lo, start, stop=False):
                nc.tensor.matmul(dst, w_hi_tile, m_hi, start=start, stop=False)
                nc.tensor.matmul(dst, w_hi_tile, m_lo, start=False, stop=False)
                return nc.tensor.matmul(dst, w_lo_tile, m_hi, start=False, stop=stop)

            def x_tile(k, h, s, x=x_hl):
                return x[:, s, k, half_of(h)]

            def gate_up_k(slot, k, h):
                for w in range(2):
                    at = slice((2 * k + w) * P, (2 * k + w + 1) * P)
                    passes(banks[:, 2 * h + w, :], w_hl[:, slot, 0, at], w_hl[:, slot, 1, at],
                           x_tile(k, h, 0), x_tile(k, h, 1), k == 0, k == KT - 1)

            def gate_up_low(slot, h):
                for w in range(2):
                    for pair in range(2 * h, 2 * h + 2):
                        c0 = (pair % 2) * PT
                        last = nc.tensor.matmul(banks[:, 2 * h + w, c0:c0 + PT],
                                                b_rows[:, slot, pair, w * P:(w + 1) * P],
                                                t_rows[:, (2 * pair + w) * PT:(2 * pair + w + 1) * PT],
                                                start=False, stop=True, skip_group_check=True)
                last.then_inc(gate_up_done, 1)

            def down_low(act_of, slot):
                for pair in range(PAIRS):
                    for s in range(2):
                        last = nc.tensor.matmul(banks[:, 4 + pair, 0:PT], down_a_cols[:, slot, pair, :],
                                                act_of(s, pair), start=False, stop=True,
                                                skip_group_check=True)
                return last

            for c in range(2 * KT):
                h, k = divmod(c, KT)
                pe.wait_ge(piece_ready, c + 1)
                gate_up_k(0, k, h)
            pe.wait_ge(gu_a_ready, 1)
            for pair in range(PAIRS):
                for w in range(2):
                    for k in range(KT):
                        for s in range(2):
                            last = nc.tensor.matmul(
                                banks[:, 4 + pair, w * PT:(w + 1) * PT],
                                gu_a_cols[:, w, k, pair * P:(pair + 1) * P],
                                x_hl[:, s, k, pair_of(pair)], start=(k == 0 and s == 0),
                                stop=(k == KT - 1 and s == 1))
            last.then_inc(low_done, 1)
            pe.wait_ge(t_ready, 1)
            for pair in range(PAIRS):
                nc.tensor.matmul(banks[:, 4 + pair, 0:PT], zeros[:, 0:P], zeros[:, :], start=True, stop=True)
            pe.wait_ge(b_ready, 1)
            for h in range(2):
                gate_up_low(0, h)

            with nc.Fori(0, (FT - 1) // 2, engines=[PE_ENGINE]) as i:
                for u in range(2):
                    ft, slot = 2 * i + (1 + u), (1 + u) % 2
                    pe.wait_ge(w_ready, ft)
                    for h in range(2):
                        pe.wait_ge(product_done, 2 * ft + (h - 1))
                        for k in range(KT):
                            gate_up_k(slot, k, h)
                        if h == 0:
                            pe.wait_ge(b_ready, ft + 1)
                        gate_up_low(slot, h)
                        if h == 0:
                            pe.wait_ge(down_a_ready, ft)
                            pe.wait_ge(act_ready, 2 * ft)
                            prev = bass.ds(ft - 1, 1)
                            down_low(lambda s, pair: act_hl[:, prev, s, pair_of(pair)].rearrange(
                                "p a t -> p (a t)"), 1 - slot)

            def down_tile(t):
                ht, k = divmod(t, FT)
                c, at = divmod(t, PER_CHUNK)
                slot = (FT + c) % 2
                cols = slice(at * P, (at + 1) * P)
                if at == 0:
                    pe.wait_ge(w_ready, FT + c)
                for h in range(2):
                    g = group_id(DOWN0, ht, h)
                    if k == 0:
                        if g >= 4:
                            pe.wait_ge(x_summed, g - 3)
                        elif h == 0:
                            pe.wait_ge(product_done, 2 * FT)
                    last = passes(banks[:, g % 4, :], w_hl[:, slot, 0, cols], w_hl[:, slot, 1, cols],
                                  act_hl[:, k, 0, half_of(h)], act_hl[:, k, 1, half_of(h)], k == 0, k == FT - 1)
                if at == PER_CHUNK - 1:
                    last.then_inc(down_chunk_used, 1)
                elif ht == KT - 1:
                    last.then_inc(act_tile_used, 1)

            def low_rows(base, ht, h, rows_of, t_base):
                g = group_id(base, ht, h)
                for pair in range(2 * h, 2 * h + 2):
                    c0 = (pair % 2) * PT
                    last = nc.tensor.matmul(banks[:, g % 4, c0:c0 + PT], rows_of(pair),
                                            t_rows[:, t_base + pair * PT:t_base + (pair + 1) * PT],
                                            start=(base == L1_0 and pair % 2 == 0), stop=True,
                                            skip_group_check=True)
                last.then_inc(group_done, 1)

            for ht in range(KT):
                for k in range(FT):
                    t = ht * FT + k
                    if t == 3:
                        pe.wait_ge(act_ready, 2 * FT)
                        pe.wait_ge(down_a_ready, FT)
                        down_low(lambda s, pair: act_hl[:, FT - 1, s, pair_of(pair)],
                                 (FT - 1) % 2).then_inc(low_done, 1)
                    down_tile(t)
                if ht == 0:
                    pe.wait_ge(t_ready, 2)
                    pe.wait_ge(b_ready, B_BLOCKS)
                for h in range(2):
                    low_rows(DOWN0, ht, h, lambda pair: b_rows[
                        :, (FT + ht // 2) % 2, pair, (ht % 2) * P:(ht % 2 + 1) * P], 0)

            def low_cols(cols, h, x):
                for pair in range(2 * h, 2 * h + 2):
                    for k in range(KT):
                        for s in range(2):
                            last = nc.tensor.matmul(banks[:, 4 + pair, 0:PT],
                                                    cols[:, k, pair * P:(pair + 1) * P],
                                                    x[:, s, k, pair_of(pair)],
                                                    start=(k == 0 and s == 0),
                                                    stop=(k == KT - 1 and s == 1))
                last.then_inc(low_done, 1)

            pe.wait_ge(late_ready, LATE["l1_a"])
            pe.wait_ge(x_ready, L1_0)
            for h in range(2):
                low_cols(l1_b_cols, h, x_hl)
            for h in range(2):
                pe.wait_ge(t_ready, 3 + h)
                for ht in range(KT):
                    pe.wait_ge(x_summed, group_id(L1_0, ht, h) - 3)
                    low_rows(L1_0, ht, h, lambda pair: l1_a_rows[:, pair, ht * P:(ht + 1) * P], PAIRS * PT)

            pe.wait_ge(late_ready, LATE["l2_b"])
            for h in range(2):
                pe.wait_ge(x_ready, L1_0 + KT * (h + 1))
                for pair in range(2 * h, 2 * h + 2):
                    for v in range(2):
                        for k in range(KT):
                            for s in range(2):
                                last = nc.tensor.matmul(banks[:, 4 + pair, v * PT:(v + 1) * PT],
                                                        l2_a_cols[:, k, pair, v, :],
                                                        x_hl[:, s, k, pair_of(pair)],
                                                        start=(k == 0 and s == 0),
                                                        stop=(k == KT - 1 and s == 1))
                last.then_inc(low_done, 1)
                for ht in range(KT):
                    g = group_id(L2_0, ht, h)
                    pe.wait_ge(x_summed, g - 3)
                    for k in range(KT):
                        cols = slice(ht * P, (ht + 1) * P)
                        passes(banks[:, g % 4, :], l2_w_hl[:, 0, k, cols], l2_w_hl[:, 1, k, cols],
                               x_tile(k, h, 0), x_tile(k, h, 1), k == 0, k == KT - 1)
                    pe.wait_ge(t_ready, 5 + h)
                    nc.tensor.matmul(banks[:, g % 4, :], l2_b_rows[:, ht * P:(ht + 1) * P],
                                     t_rows[:, half_of(h)], start=False, stop=True,
                                     skip_group_check=True).then_inc(group_done, 1)

            pe.wait_ge(late_ready, LATE["l3_b"])
            for h in range(2):
                pe.wait_ge(x_ready, L2_0 + KT * (h + 1))
                low_cols(l3_a_cols, h, x3_hl)
                for ht in range(KT):
                    g = group_id(L3_0, ht, h)
                    pe.wait_ge(x_summed, g - 3)
                    for k in range(KT):
                        cols = slice(ht * P, (ht + 1) * P)
                        passes(banks[:, g % 4, :], l3_w_hl[:, 0, k, cols], l3_w_hl[:, 1, k, cols],
                               x_tile(k, h, 0, x3_hl), x_tile(k, h, 1, x3_hl), k == 0, k == KT - 1)
                    pe.wait_ge(t_ready, 7 + h)
                    low_rows(L3_0, ht, h, lambda pair: l3_b_rows[:, pair, ht * P:(ht + 1) * P], PAIRS * PT)


def kernel(**inputs):
    import numpy as np
    import concourse.bacc as bacc
    from concourse.bass_utils import run_bass_kernel_spmd

    a = {k: np.asarray(v) for k, v in inputs.items()}

    def pad_f(m, axis):
        widths = [(0, 0)] * m.ndim
        widths[axis] = (0, FPAD - FFN)
        return np.pad(m, widths)

    def cols_table(t):
        n, r, f = t.shape
        return t.reshape(n, r, f // P, P).transpose(0, 3, 2, 1)

    def gate_up_tiles(w):
        return pad_f(w, 0).reshape(FT, P, KT, P).transpose(0, 3, 2, 1)

    gu = np.stack([gate_up_tiles(a["L0_cond_W_gate"]), gate_up_tiles(a["L0_cond_W_up"])], 3)
    gu = gu.reshape(FT, P, CHUNK)
    down = pad_f(a["L0_cond_W_down"], 1).reshape(KT, P, FT, P).transpose(0, 2, 3, 1)
    down = np.pad(down.reshape(DOWN_TILES, P, P),
                  [(0, DOWN_CHUNKS * PER_CHUNK - DOWN_TILES), (0, 0), (0, 0)])
    down = down.reshape(DOWN_CHUNKS, PER_CHUNK, P, P).transpose(0, 2, 1, 3).reshape(DOWN_CHUNKS, P, CHUNK)

    def rows_ffn(t):
        return pad_f(t[0], 1).reshape(-1, FT, P, RANK).transpose(0, 1, 3, 2)

    up_b = np.stack([rows_ffn(a["L0_cond_B_gate"]), rows_ffn(a["L0_cond_B_up"])], 3)
    up_b = up_b.reshape(-1, FT, RANK, 2 * P)
    down_b = a["L0_cond_B_down"][0].reshape(-1, KT // 2, 2 * P, RANK).transpose(0, 1, 3, 2)

    def square(w):
        return w.T.reshape(KT, P, HID).transpose(1, 0, 2).reshape(P, KT * HID)

    sign = np.zeros((P, 2), np.float32)
    sign[2::4, 0] = -1.0
    sign[1::4, 1] = -1.0
    data = {
        "x_t": a["x"].reshape(TOK, HID).T.reshape(KT, P, TOK),
        "weights": np.concatenate([gu, down], 0),
        "indices": np.concatenate([a["itok_B_2_6"], a["itok_B_3_7"], a["itok_B_0_2"],
                                   a["itok_B_6_15"]]).reshape(1, 4 * BATCH),
        "gu_a": np.stack([cols_table(a["L0_cond_A_gate"][0]), cols_table(a["L0_cond_A_up"][0])],
                         2).reshape(ADAPTERS["l0"], P, 2 * KT * RANK),
        "up_b": np.concatenate([up_b, down_b], 1),
        "down_a": cols_table(pad_f(a["L0_cond_A_down"][0], 2)).reshape(ADAPTERS["l0"], P, FT * RANK),
        "l1_b": cols_table(a["L1_cond_B"]).reshape(ADAPTERS["l1"], P, KT * RANK),
        "l1_a": a["L1_cond_A"].transpose(0, 2, 1),
        "l2_w": square(a["L2_cond_W"]),
        "l2_a": cols_table(a["L2_cond_lora_A"].transpose(0, 2, 1)),
        "l2_b": np.repeat(a["L2_cond_lora_B_w"].T, COPIES, 0),
        "l3_w": square(a["L3_cond_base_weight"]),
        "l3_a": cols_table(a["L3_cond_lora_A_w"]).reshape(ADAPTERS["l3"], P, KT * RANK),
        "l3_b": a["L3_cond_lora_B_w"].transpose(0, 2, 1),
        "bias": a["L3_cond_base_bias"].reshape(KT, P).T,
        "row_signs": sign,
    }
    nc = bacc.Bacc("TRN2", target_bir_lowering=False, num_devices=1)
    arrays, args = {}, []
    for name, v in data.items():
        arrays[name] = np.ascontiguousarray(v)
        args.append(nc.dram_tensor(name, v.shape, mybir.dt.from_np(v.dtype), kind="ExternalInput").ap())
    out_t = nc.dram_tensor("out_t", (KT, P, TOK), F32, kind="ExternalOutput").ap()
    lora_chain_kernel(nc, *args, out_t)
    r = run_bass_kernel_spmd(nc, [arrays], core_ids=[0])
    got = r.results[0]["out_t"]
    return np.ascontiguousarray(got.reshape(HID, TOK).T).reshape(BATCH, SEQ, HID)
```

```python
from contextlib import ExitStack

import concourse.bass as bass
from concourse import mybir

F32 = mybir.dt.float32
F32R = mybir.dt.float32r
ALU = mybir.AluOpType
ACT = mybir.ActivationFunctionType
DVE_ENGINE = mybir.EngineType.DVE
ACT_ENGINE = mybir.EngineType.Activation
PE_ENGINE = mybir.EngineType.PE
SP_ENGINE = mybir.EngineType.SP
POOL_ENGINE = mybir.EngineType.Pool

P = 128
BATCH, SEQ, HID, FFN = 8, 128, 512, 1376
TOK = BATCH * SEQ
KT = HID // P
FT = -(-FFN // P)
FPAD = FT * P
HALF = TOK // 2
PAIRS = BATCH // 2
PT = 2 * SEQ
RANK = 16
COPIES = 4
DOWN_TILES = KT * FT
PER_CHUNK = 8
CHUNK = PER_CHUNK * P
DOWN_CHUNKS = -(-DOWN_TILES // PER_CHUNK)
CHUNKS = FT + DOWN_CHUNKS
B_BLOCKS = FT + KT // 2
L0_SCALE, L2_SCALE = 0.5, 0.5
ADAPTERS = {"l0": 16, "l1": 8, "l2": 5, "l3": 32}


def lora_chain_kernel(nc, x_t, weights, indices, gu_a, up_b, down_a, l1_b, l1_a, l2_w, l2_a, l2_b,
                      l3_w, l3_a, l3_b, bias, row_signs, out):
    ctx = ExitStack()
    with ctx:
        def sb(name, shape, dt=F32):
            return ctx.enter_context(nc.sbuf_tensor(name, shape, dt))

        def sem(name):
            return ctx.enter_context(nc.semaphore(name))

        act_hl = sb("act_hl", [P, FT, 2, TOK], F32R)
        x_hl = sb("x_hl", [P, 2, KT, TOK], F32R)
        w_hl = sb("w_hl", [P, 2, 2, CHUNK], F32R)
        b_rows = sb("b_rows", [P, 2, PAIRS, 2 * P], F32R)
        down_a_cols = sb("down_a_cols", [P, 2, PAIRS, P], F32R)
        t_rows = sb("t_rows", [P, 2 * PAIRS * PT], F32R)
        zeros = sb("zeros", [P, PT], F32R)

        def freed(tile, n, h):
            return act_hl[:, tile:tile + n, :, h * HALF:(h + 1) * HALF].rearrange("p a s t -> p (a s) t")

        gu_a_cols = act_hl[:, 9:11, :, :].rearrange("p a b c -> p (a b c)").rearrange(
            "p (w k c) -> p w k c", w=2, k=KT)
        l1_b_cols = [down_a_cols[:, k, :, :].rearrange("p a c -> p (a c)") for k in range(2)] + [
            freed(0, 1, 0)[:, s, :] for s in range(2)]
        l1_a_rows = freed(1, 2, 0)
        l2_w_hl = act_hl[:, 3:3 + KT, :, 0:HALF]
        l2_a_cols = act_hl[:, 0:KT, 0, HALF:TOK].rearrange("p k (a c) -> p k a c", a=PAIRS)
        l2_b_rows = act_hl[:, 4, 0, HALF:TOK]
        l3_b_rows = l1_a_rows
        x3_hl = act_hl[:, 7:7 + KT, :, :].rearrange("p k s t -> p s k t")
        l3_w_hl = w_hl[:, :, :, :].rearrange("p a b c -> p (a b c)").rearrange(
            "p (k s o) -> p k s o", s=2, k=KT)
        l3_a_cols = b_rows[:, :, :, :].rearrange("p a b c -> p (a b c)").rearrange(
            "p (k c) -> p k c", k=KT)
        l3_a_cols = [l3_a_cols[:, k, :] for k in range(KT)]

        x_res = sb("x_res", [P, KT, TOK])
        w_raw = sb("w_raw", [P, 2, CHUNK])
        b_raw = sb("b_raw", [P, PAIRS, 2 * P])
        down_a_raw = sb("down_a_raw", [P, BATCH, FT, RANK])
        low_raw = sb("low_raw", [P, 4 * HID])
        silu_out = sb("silu_out", [P, 4 * HID])
        bias_col = sb("bias_col", [P, KT])
        sign_col = sb("sign_col", [P, 3])
        t_sign, b_sign = sign_col[:, 0:1], sign_col[:, 1:2]
        t_sign_half = sb("t_sign_half", [P, 1])
        scratch = sb("scratch", [P, 1])

        down_a_flat = down_a_raw[:, :, :, :].rearrange("p a b c -> p (a b c)")
        gu_a_raw = low_raw[:, 0:1024].rearrange("p (b w k r) -> p b w k r", b=BATCH, w=2, k=KT)
        l1_b_raw = down_a_flat[:, 0:512].rearrange("p (b k r) -> p b k r", b=BATCH, k=KT)
        l2_b_raw = down_a_flat[:, 512:1024]
        l1_a_raw = low_raw[:, :].rearrange("p (r o) -> p r o", r=PAIRS)
        b_raw_at = [b_raw[:, :, :], silu_out[:, 2 * HID:].rearrange("p (a c) -> p a c", a=PAIRS)]
        l2_w_raw = silu_out[:, :].rearrange("p (k o) -> p k o", k=KT)
        l2_a_raw = b_raw[:, :, :].rearrange("p a b -> p (a b)").rearrange(
            "p (k a c) -> p k a c", k=KT, a=PAIRS)
        l3_w_raw = w_raw[:, :, :].rearrange("p a b -> p (a b)").rearrange("p (k o) -> p k o", k=KT)
        l3_a_raw = l1_b_raw
        l3_b_raw = l1_a_raw

        banks = ctx.enter_context(nc.psum_tensor("banks", [P, 8, 512], F32))

        piece_landed = [sem(f"piece_landed{c}") for c in range(2 * KT)]
        signs_landed = sem("signs_landed")
        bias_landed = sem("bias_landed")
        piece_hi = sem("piece_hi")
        piece_ready = sem("piece_ready")
        w_landed = [sem(f"w_landed{s}") for s in range(2)]
        w_hi = sem("w_hi")
        w_ready = sem("w_ready")
        b_landed = [sem(f"b_landed{s}") for s in range(2)]
        b_signed = sem("b_signed")
        b_ready = sem("b_ready")
        gu_a_landed = [sem(f"gu_a_landed{s}") for s in range(2)]
        gu_a_hi = sem("gu_a_hi")
        gu_a_ready = sem("gu_a_ready")
        down_a_landed = sem("down_a_landed")
        down_a_hi = sem("down_a_hi")
        down_a_ready = sem("down_a_ready")
        scratch_zeroed = sem("scratch_zeroed")
        zeros_set = sem("zeros_set")
        t_zeroed = sem("t_zeroed")
        sign_scaled = sem("sign_scaled")
        low_done = sem("low_done")
        t_signed = sem("t_signed")
        t_ready = sem("t_ready")
        gate_up_done = sem("gate_up_done")
        silu_done = sem("silu_done")
        product_done = sem("product_done")
        act_hi = sem("act_hi")
        act_ready = sem("act_ready")
        down_chunk_used = sem("down_chunk_used")
        act_tile_used = sem("act_tile_used")
        group_done = sem("group_done")
        x_summed = sem("x_summed")
        x_hi = sem("x_hi")
        x_ready = sem("x_ready")
        late_landed = {n: sem(f"{n}_landed") for n in
                       ("l2_w", "l1_b", "l1_a", "l2_a", "l2_b", "l3_w", "l3_a", "l3_b")}
        late_hi = sem("late_hi")
        late_ready = sem("late_ready")
        out_stored = sem("out_stored")
        LATE = {"l1_b": 1, "l1_a": 2, "l2_w": 3, "l2_a": 4, "l2_b": 5, "l3_w": 5 + KT,
                "l3_a": 5 + 2 * KT, "l3_b": 5 + 2 * KT + PAIRS}
        DOWN, L1, L2, L3 = range(4)
        ORDER = [(DOWN, ht, h) for ht in range(KT - 1) for h in range(2)] + [(DOWN, KT - 1, 0)] + \
            [(L1, ht, 0) for ht in range(KT)] + [(DOWN, KT - 1, 1)] + [(L1, ht, 1) for ht in range(KT)] + \
            [(layer, ht, h) for layer in (L2, L3) for h in range(2) for ht in range(KT)]
        BANKS = [0, 1, 2, 3, 4, 0, 1] + [3, 4, 0, 1] + [2] + [4, 0, 1, 2] + [7, 3, 4, 0, 1, 2, 7, 3] + \
            [4, 0, 1, 2, 7, 3, 4, 0]
        PLACE = {g: n for n, g in enumerate(ORDER)}
        LOW_BANK, L2_LOW_BANK = 5, 6

        def count(layer, ht, h):
            return PLACE[(layer, ht, h)] + 1

        def bank(layer, ht, h):
            return banks[:, BANKS[PLACE[(layer, ht, h)]], :]

        def bank_free(layer, ht, h):
            n = PLACE[(layer, ht, h)]
            return max([m + 1 for m in range(n) if BANKS[m] == BANKS[n]], default=0)

        def half_of(h):
            return slice(h * HALF, (h + 1) * HALF)

        def pair_of(pair):
            return slice(pair * PT, (pair + 1) * PT)

        def cols_view(cols):
            v = cols.rearrange("p (b r g) -> p b r g", r=RANK, g=COPIES)
            return v[:, :, :, 0:3], v[:, :, :, 3]

        def l2_t(quarter, h, blk):
            return t_rows[32 * quarter:32 * quarter + 32, half_of(h)].rearrange(
                "p (a t) -> p a t", t=PT)[:, :, blk * SEQ:(blk + 1) * SEQ]

        def l2_low(row, blk):
            return banks[row:row + 32, L2_LOW_BANK, :].rearrange(
                "p (a t) -> p a t", t=PT)[:, :, blk * SEQ:(blk + 1) * SEQ]

        block = ctx.enter_context(nc.Block())

        def load_adapters(eng, engine_type, layer, name):
            at = layer * BATCH
            return nc.values_load_multi_w_load_instructions(
                indices[0:1, at:at + BATCH], engines=[engine_type], min_val=0,
                max_val=ADAPTERS[name] - 1)[1]

        def gather_rows(eng, table, adapter, raw, landed):
            for b in range(BATCH):
                src = table(adapter[b])
                rows = slice(64 * (b % 2), 64 * (b % 2) + 64)
                eng.dma_start(raw[rows, b // 2, :], src.unsqueeze(1).broadcast_to(
                    [RANK, COPIES, src.shape[-1]])).then_inc(landed, 16)

        def gather_cols(table, adapter, raw_of, landed, eng, batches=range(BATCH)):
            for b in batches:
                src = table[bass.ds(adapter[b], 1)]
                src = src.rearrange("a p k r -> (a p) k r") if len(src.shape) == 4 else \
                    src.rearrange("a p c -> (a p) c")
                eng.dma_start(raw_of(b), src).then_inc(landed, 16)

        def gu_a_raw_of(b):
            return gu_a_raw[:, b, :, :, :].rearrange("p w k r -> p (w k r)")

        @block.sync
        def _(sp):
            for c in range(2 * KT):
                h, k = divmod(c, KT)
                if h == 0:
                    sp.dma_start(w_raw[:, 0, k * 256:(k + 1) * 256],
                                 weights[0, :, k * 256:(k + 1) * 256]).then_inc(piece_landed[c], 16)
                sp.dma_start(x_res[:, k, half_of(h)], x_t[k, :, half_of(h)]).then_inc(piece_landed[c], 16)
            sp.dma_start(w_raw[:, 1, :], weights[1]).then_inc(w_landed[1], 16)
            l0 = load_adapters(sp, SP_ENGINE, 0, "l0")

            def b_block(n):
                return lambda a: up_b[bass.ds(a, 1), n].rearrange("a r c -> (a r) c")

            for n in range(2):
                gather_rows(sp, b_block(n), l0, b_raw_at[n], b_landed[n])
            sp.wait_ge(piece_ready, KT)
            sp.dma_start(w_raw[:, 0, :], weights[2]).then_inc(w_landed[0], 16)
            with nc.Fori(0, (FT - 1) // 2, engines=[SP_ENGINE]) as i:
                for u in range(2):
                    sp.wait_ge(b_ready, 2 * i + (1 + u))
                    gather_rows(sp, lambda a: up_b[bass.ds(a, 1), bass.ds(2 * i + (2 + u), 1)].rearrange(
                        "a n r c -> (a n r) c"), l0, b_raw_at[u], b_landed[u])
                    sp.wait_ge(w_ready, 2 * i + (1 + u))
                    sp.dma_start(w_raw[:, (1 + u) % 2, :], weights[bass.ds(2 * i + (3 + u), 1)].rearrange(
                        "a p c -> (a p) c")).then_inc(w_landed[(1 + u) % 2], 16)
            sp.wait_ge(b_ready, B_BLOCKS - 2)
            gather_rows(sp, b_block(B_BLOCKS - 1), l0, b_raw_at[0], b_landed[0])
            for n in range(FT + 2, CHUNKS):
                sp.wait_ge(w_ready, n - 2)
                sp.dma_start(w_raw[:, n % 2, :], weights[n]).then_inc(w_landed[n % 2], 16)
                if n == FT + 2:
                    sp.wait_ge(act_ready, 2 * FT)
                    sp.wait_ge(b_ready, B_BLOCKS - 1)
                    sp.dma_start(silu_out[:, :], l2_w).then_inc(late_landed["l2_w"], 16)
                    sp.wait_ge(down_a_ready, FT)
                    sp.dma_start(l2_b_raw, l2_b).then_inc(late_landed["l2_b"], 16)
            sp.wait_ge(w_ready, CHUNKS - 1)
            sp.dma_start(w_raw[:, :, :].rearrange("p a b -> p (a b)"), l3_w).then_inc(
                late_landed["l3_w"], 16)
            for h in range(2):
                for ht in range(KT):
                    sp.wait_ge(x_summed, count(L3, ht, h))
                    sp.dma_start(out[ht, :, half_of(h)], x_res[:, ht, half_of(h)]).then_inc(out_stored, 16)
            sp.wait_ge(out_stored, 16 * 2 * KT)

        @block.gpsimd
        def _(pool):
            l0 = load_adapters(pool, POOL_ENGINE, 0, "l0")
            gather_cols(gu_a, l0, gu_a_raw_of, gu_a_landed[0], pool, range(BATCH // 2))
            pool.dma_start(sign_col[:, :], row_signs).then_inc(signs_landed, 16)
            pool.dma_start(bias_col[:, :], bias).then_inc(bias_landed, 16)
            gather_cols(down_a, l0, lambda b: down_a_raw[:, b, :, :].rearrange(
                "p f r -> p (f r)"), down_a_landed, pool)
            l1 = load_adapters(pool, POOL_ENGINE, 1, "l1")
            pool.wait_ge(gu_a_ready, 1)
            gather_rows(pool, lambda a: l1_a[bass.ds(a, 1)].rearrange("a r o -> (a r) o"), l1, l1_a_raw,
                        late_landed["l1_a"])
            pool.wait_ge(down_a_ready, FT)
            gather_cols(l1_b, l1, lambda b: l1_b_raw[:, b, :, :].rearrange("p k r -> p (k r)"),
                        late_landed["l1_b"], pool)
            l2 = load_adapters(pool, POOL_ENGINE, 2, "l2")
            pool.wait_ge(b_ready, B_BLOCKS)
            gather_cols(l2_a, l2, lambda b: l2_a_raw[:, :, b // 2, 32 * (b % 2):32 * (b % 2) + 32], late_landed["l2_a"], pool)
            l3 = load_adapters(pool, POOL_ENGINE, 3, "l3")
            pool.wait_ge(late_ready, LATE["l1_b"])
            gather_cols(l3_a, l3, lambda b: l3_a_raw[:, b, :, :].rearrange("p k r -> p (k r)"),
                        late_landed["l3_a"], pool)
            pool.wait_ge(late_ready, LATE["l1_a"])
            gather_rows(pool, lambda a: l3_b[bass.ds(a, 1)].rearrange("a r o -> (a r) o"), l3, l3_b_raw,
                        late_landed["l3_b"])

        @block.scalar
        def _(act):
            def hi(dst, src):
                return nc.scalar.activation(dst, src, ACT.Copy)

            def signed(dst, src, sign):
                return nc.scalar.activation(dst, src, ACT.Copy, scale=sign)

            act.wait_ge(scratch_zeroed, 1)
            nc.scalar.activation(scratch[:, :], scratch[:, :], ACT.Silu)
            l0 = load_adapters(act, ACT_ENGINE, 0, "l0")
            for c in range(2 * KT):
                h, k = divmod(c, KT)
                act.wait_ge(piece_landed[c], 32 if h == 0 else 16)
                if h == 0:
                    hi(w_hl[:, 0, 0, k * 256:(k + 1) * 256], w_raw[:, 0, k * 256:(k + 1) * 256])
                hi(x_hl[:, 0, k, half_of(h)], x_res[:, k, half_of(h)]).then_inc(piece_hi, 1)
                if c == 0:
                    gather_cols(gu_a, l0, gu_a_raw_of, gu_a_landed[1], act, range(BATCH // 2, BATCH))
            for landed in gu_a_landed:
                act.wait_ge(landed, 16 * BATCH // 2)
            for w in range(2):
                for k in range(KT):
                    his, _ = cols_view(gu_a_cols[:, w, k, :])
                    hi(his, gu_a_raw[:, :, w, k, :].unsqueeze(3).broadcast_to(
                        [P, BATCH, RANK, 3])).then_inc(gu_a_hi, 1)
            act.wait_ge(signs_landed, 16)
            act.wait_ge(sign_scaled, 1)

            def b_block_signed(slot, landed):
                act.wait_ge(b_landed[slot], landed)
                signed(b_rows[:, slot, :, :], b_raw_at[slot], b_sign).then_inc(b_signed, 1)

            def down_a_split(ft, slot):
                his, _ = cols_view(down_a_cols[:, slot, :, :].rearrange("p a c -> p (a c)"))
                hi(his, down_a_raw[:, :, ft, :].unsqueeze(3).broadcast_to(
                    [P, BATCH, RANK, 3])).then_inc(down_a_hi, 1)

            def t_split(row_half, dst, src, sign):
                rows = slice(64 * row_half, 64 * row_half + 64)
                return signed(dst[rows], src[rows], sign[rows])

            def ffn_half(ft, h, step, first):
                act.wait_ge(gate_up_done, step + 1)
                if not first:
                    act.wait_ge(act_ready, step - 1)
                nc.scalar.activation(silu_out[:, half_of(h)], banks[:, 2 * h, :], ACT.Silu).then_inc(
                    silu_done, 1)

            def ffn_hi(ft, h, step):
                act.wait_ge(product_done, step + 1)
                hi(act_hl[:, ft, 0, half_of(h)], silu_out[:, half_of(h)]).then_inc(act_hi, 1)

            def weights_hi(slot, landed):
                act.wait_ge(w_landed[slot], landed)
                hi(w_hl[:, slot, 0, :], w_raw[:, slot, :]).then_inc(w_hi, 1)

            b_block_signed(0, 16 * BATCH)
            act.wait_ge(t_zeroed, 1)
            for h in range(2):
                act.wait_ge(low_done, 1 + h)
                gu_low = banks[:, 4 + 2 * h:6 + 2 * h, :].rearrange("p a (w t) -> p (a w) t", w=2)
                gu_t = t_rows[:, :].rearrange("p (a t) -> p a t", t=PT)[:, 4 * h:4 * h + 4, :]
                for r in range(2):
                    at = slice(r * SEQ, (r + 1) * SEQ)
                    last = t_split(r, gu_t[:, :, at], gu_low[:, :, at], t_sign_half)
                last.then_inc(t_signed, 1)
            weights_hi(1, 16)
            act.wait_ge(down_a_landed, 16 * BATCH)
            ffn_half(0, 0, 0, True)
            ffn_hi(0, 0, 0)
            ffn_half(0, 1, 1, True)
            b_block_signed(1, 16 * BATCH)
            down_a_split(0, 0)
            ffn_hi(0, 1, 1)
            with nc.Fori(0, (FT - 1) // 2, engines=[ACT_ENGINE]) as i:
                for u in range(2):
                    ft, slot = 2 * i + (1 + u), (1 + u) % 2
                    ft_at = bass.ds(ft, 1)

                    def act_at(h):
                        return act_hl[:, ft_at, 0, half_of(h)].rearrange("p a t -> p (a t)")

                    for h in range(2):
                        step = 4 * i + (2 + 2 * u + h)
                        act.wait_ge(gate_up_done, step + 1)
                        act.wait_ge(act_ready, step - 1)
                        nc.scalar.activation(silu_out[:, half_of(h)], banks[:, 2 * h, :],
                                             ACT.Silu).then_inc(silu_done, 1)
                        if h == 0:
                            act.wait_ge(w_landed[1 - slot], 16 * i + 16 * (1 + u))
                            hi(w_hl[:, 1 - slot, 0, :], w_raw[:, 1 - slot, :]).then_inc(w_hi, 1)
                        else:
                            act.wait_ge(b_landed[1 - slot], 16 * BATCH * i + 16 * BATCH * 2)
                            signed(b_rows[:, 1 - slot, :, :], b_raw_at[1 - slot], b_sign).then_inc(
                                b_signed, 1)
                            his, _ = cols_view(down_a_cols[:, slot, :, :].rearrange("p a c -> p (a c)"))
                            hi(his, down_a_raw[:, :, ft_at, :].rearrange("p b f r -> p b (f r)").unsqueeze(
                                3).broadcast_to([P, BATCH, RANK, 3])).then_inc(down_a_hi, 1)
                        act.wait_ge(product_done, step + 1)
                        hi(act_at(h), silu_out[:, half_of(h)]).then_inc(act_hi, 1)
            weights_hi(0, 16 * (FT + 1) // 2)
            act.wait_ge(low_done, 3)
            down_t = t_rows[:, 0:PAIRS * PT].rearrange("p (a t) -> p a t", t=PT)
            for r in range(2):
                at = slice(r * SEQ, (r + 1) * SEQ)
                last = t_split(r, down_t[:, :, at], banks[:, 4:8, at], t_sign_half)
            last.then_inc(t_signed, 1)

            def down_chunk_hi(c):
                act.wait_ge(down_chunk_used, c - 1)
                n = FT + c
                slot = n % 2
                act.wait_ge(w_landed[slot], 16 * ((n + 1) // 2))
                m = min(PER_CHUNK, DOWN_TILES - c * PER_CHUNK) * P
                hi(w_hl[:, slot, 0, 0:m], w_raw[:, slot, 0:m]).then_inc(w_hi, 1)

            def x_hi_part(base, ht, h):
                act.wait_ge(x_summed, count(base, ht, h))
                dst = x3_hl if base == L2 else x_hl
                hi(dst[:, 0, ht, half_of(h)], x_res[:, ht, half_of(h)]).then_inc(x_hi, 1)

            def cols_hi(cols, raw):
                his, _ = cols_view(cols)
                return hi(his, raw.unsqueeze(3).broadcast_to([P, BATCH, RANK, 3]))

            def rows_signed(name, rows, raw, gathers):
                act.wait_ge(late_landed[name], 16 * gathers)
                signed(rows, raw, b_sign).then_inc(late_hi, 1)

            def matrix_hi(name, dst, raw):
                act.wait_ge(late_landed[name], 16)
                hi(dst[:, :, 0, :], raw).then_inc(late_hi, 1)

            def low_signed(event, h):
                act.wait_ge(low_done, event)
                dst = t_rows[:, PAIRS * PT + h * HALF:PAIRS * PT + (h + 1) * HALF].rearrange(
                    "p (a t) -> p a t", t=PT)
                src = banks[:, LOW_BANK, :].rearrange("p (a t) -> p a t", t=PT)
                for r in range(2):
                    at = slice(r * SEQ, (r + 1) * SEQ)
                    last = t_split(r, dst[:, :, at], src[:, :, at], t_sign)
                last.then_inc(t_signed, 1)

            def l2_low_hi(event, h):
                act.wait_ge(low_done, event)
                for q in (0, 1, 3):
                    for blk in range(2):
                        src = 32 * blk + (64 if q == 3 else 0)
                        last = nc.scalar.activation(l2_t(q, h, blk), l2_low(src, blk), ACT.Copy,
                                                    scale=L2_SCALE)
                last.then_inc(t_signed, 1)

            down_chunk_hi(2)
            b_block_signed(0, 16 * BATCH * (B_BLOCKS // 2 + 1))
            for h in range(2):
                x_hi_part(DOWN, 0, h)
            down_chunk_hi(3)
            for h in range(2):
                x_hi_part(DOWN, 1, h)
            down_chunk_hi(4)
            down_chunk_hi(5)
            for h in range(2):
                x_hi_part(DOWN, 2, h)
            act.wait_ge(late_landed["l1_b"], 16 * BATCH)
            for k in range(KT):
                if k == 2:
                    act.wait_ge(act_tile_used, 1)
                last = cols_hi(l1_b_cols[k], l1_b_raw[:, :, k, :])
            last.then_inc(late_hi, 1)
            act.wait_ge(act_tile_used, 3)
            rows_signed("l1_a", l1_a_rows, l1_a_raw, BATCH)
            act.wait_ge(act_tile_used, 7)
            matrix_hi("l2_w", l2_w_hl, l2_w_raw)
            x_hi_part(DOWN, 3, 0)
            act.wait_ge(late_landed["l2_a"], 16 * BATCH)
            act.wait_ge(act_tile_used, FT + 4)
            hi(l2_a_cols[:, :, :, 0:64], l2_a_raw).then_inc(late_hi, 1)
            low_signed(4, 0)
            act.wait_ge(act_tile_used, FT + 5)
            act.wait_ge(late_landed["l2_b"], 16)
            signed(l2_b_rows, l2_b_raw, sign_col[:, 2:3]).then_inc(late_hi, 1)
            for ht in range(KT):
                x_hi_part(L1, ht, 0)
            x_hi_part(DOWN, 3, 1)
            l2_low_hi(5, 0)
            low_signed(6, 1)
            act.wait_ge(late_landed["l3_w"], 16)
            for ht in range(KT):
                x_hi_part(L1, ht, 1)
                hi(l3_w_hl[:, ht, 0, :], l3_w_raw[:, ht, :]).then_inc(late_hi, 1)
            act.wait_ge(late_landed["l3_a"], 16 * BATCH)
            act.wait_ge(late_landed["l3_b"], 16 * BATCH)
            for ht in range(KT):
                x_hi_part(L2, ht, 0)
                if ht == 1:
                    l2_low_hi(7, 1)
                cols_hi(l3_a_cols[ht], l3_a_raw[:, :, ht, :]).then_inc(late_hi, 1)
            act.wait_ge(group_done, count(L1, KT - 1, 1))
            for ht in range(KT):
                signed(l3_b_rows[:, ht, :], l3_b_raw[:, ht, :], b_sign).then_inc(late_hi, 1)
                if ht == KT - 1:
                    low_signed(8, 0)
                x_hi_part(L2, ht, 1)
            low_signed(9, 1)

        @block.vector
        def _(dve):
            def lo(dst, src, hi_part):
                return nc.vector.tensor_tensor(dst, src, hi_part.bitcast(F32), ALU.subtract)

            def add_signed(rows, raw):
                return nc.vector.tensor_tensor(rows, raw, rows.bitcast(F32), ALU.add)

            nc.vector.memset(scratch[:, :], 0.0).then_inc(scratch_zeroed, 1)
            nc.vector.memset(zeros[:, :].bitcast(F32), 0.0).then_inc(zeros_set, 1)
            nc.vector.memset(t_rows[:, :].bitcast(F32), 0.0).then_inc(t_zeroed, 1)
            for c in range(2 * KT):
                h, k = divmod(c, KT)
                dve.wait_ge(piece_hi, c + 1)
                if h == 0:
                    at = slice(k * 256, (k + 1) * 256)
                    lo(w_hl[:, 0, 1, at], w_raw[:, 0, at], w_hl[:, 0, 0, at])
                lo(x_hl[:, 1, k, half_of(h)], x_res[:, k, half_of(h)], x_hl[:, 0, k, half_of(h)]).then_inc(
                    piece_ready, 1)

            def cols_lo(cols, raw):
                his, los = cols_view(cols)
                return lo(los, raw, his[:, :, :, 0])

            dve.wait_ge(signs_landed, 16)
            nc.vector.tensor_scalar(t_sign_half[:, :], t_sign, L0_SCALE, None, ALU.mult).then_inc(
                sign_scaled, 1)
            for w in range(2):
                for k in range(KT):
                    dve.wait_ge(gu_a_hi, w * KT + k + 1)
                    last = cols_lo(gu_a_cols[:, w, k, :], gu_a_raw[:, :, w, k, :])
            last.then_inc(gu_a_ready, 1)

            def b_block_add(n, slot):
                dve.wait_ge(b_signed, n + 1)
                add_signed(b_rows[:, slot, :, :], b_raw_at[slot]).then_inc(b_ready, 1)

            def t_add(rows, dst, src, scale):
                return nc.vector.scalar_tensor_tensor(out=dst[rows], in0=src[rows], scalar=scale,
                                                      in1=dst[rows].bitcast(F32), op0=ALU.mult,
                                                      op1=ALU.add)

            b_block_add(0, 0)
            for h in range(2):
                dve.wait_ge(t_signed, 1 + h)
                gu_low = banks[:, 4 + 2 * h:6 + 2 * h, :].rearrange("p a (w t) -> p (a w) t", w=2)
                gu_t = t_rows[:, :].rearrange("p (a t) -> p a t", t=PT)[:, 4 * h:4 * h + 4, :]
                for r in range(2):
                    at = slice(r * SEQ, (r + 1) * SEQ)
                    last = t_add(slice(64 * r, 64 * r + 64), gu_t[:, :, at], gu_low[:, :, at], L0_SCALE)
                last.then_inc(t_ready, 1)

            def weights_lo(slot, count, m=CHUNK):
                dve.wait_ge(w_hi, count)
                lo(w_hl[:, slot, 1, 0:m], w_raw[:, slot, 0:m], w_hl[:, slot, 0, 0:m]).then_inc(w_ready, 1)

            def product(h, step):
                dve.wait_ge(silu_done, step + 1)
                nc.vector.tensor_tensor(silu_out[:, half_of(h)], banks[:, 2 * h + 1, :],
                                        silu_out[:, half_of(h)], ALU.mult).then_inc(product_done, 1)

            weights_lo(1, 1)
            for h in range(2):
                product(h, h)
                if h == 1:
                    b_block_add(1, 1)
                    dve.wait_ge(down_a_hi, 1)
                    cols_lo(down_a_cols[:, 0, :, :].rearrange("p a c -> p (a c)"),
                            down_a_raw[:, :, 0, :]).then_inc(down_a_ready, 1)
                dve.wait_ge(act_hi, h + 1)
                lo(act_hl[:, 0, 1, half_of(h)], silu_out[:, half_of(h)],
                   act_hl[:, 0, 0, half_of(h)]).then_inc(act_ready, 1)
            with nc.Fori(0, (FT - 1) // 2, engines=[DVE_ENGINE]) as i:
                for u in range(2):
                    ft, slot = 2 * i + (1 + u), (1 + u) % 2
                    ft_at = bass.ds(ft, 1)
                    for h in range(2):
                        step = 4 * i + (2 + 2 * u + h)
                        dve.wait_ge(silu_done, step + 1)
                        nc.vector.tensor_tensor(silu_out[:, half_of(h)], banks[:, 2 * h + 1, :],
                                                silu_out[:, half_of(h)], ALU.mult).then_inc(
                                                    product_done, 1)
                        if h == 0:
                            dve.wait_ge(w_hi, ft + 1)
                            lo(w_hl[:, 1 - slot, 1, :], w_raw[:, 1 - slot, :],
                               w_hl[:, 1 - slot, 0, :]).then_inc(w_ready, 1)
                        else:
                            dve.wait_ge(b_signed, ft + 2)
                            add_signed(b_rows[:, 1 - slot, :, :], b_raw_at[1 - slot]).then_inc(b_ready, 1)
                            dve.wait_ge(down_a_hi, ft + 1)
                            cols_lo(down_a_cols[:, slot, :, :].rearrange("p a c -> p (a c)"),
                                    down_a_raw[:, :, ft_at, :].rearrange(
                                        "p b f r -> p b (f r)")).then_inc(down_a_ready, 1)
                        dve.wait_ge(act_hi, step + 1)
                        lo(act_hl[:, ft_at, 1, half_of(h)].rearrange("p a t -> p (a t)"),
                           silu_out[:, half_of(h)],
                           act_hl[:, ft_at, 0, half_of(h)].rearrange("p a t -> p (a t)")).then_inc(
                               act_ready, 1)
            weights_lo(0, FT + 1)
            dve.wait_ge(t_signed, 3)
            down_t = t_rows[:, 0:PAIRS * PT].rearrange("p (a t) -> p a t", t=PT)
            for r in range(2):
                at = slice(r * SEQ, (r + 1) * SEQ)
                last = t_add(slice(64 * r, 64 * r + 64), down_t[:, :, at], banks[:, 4:8, at], L0_SCALE)
            last.then_inc(t_ready, 1)

            def down_chunk_lo(c):
                weights_lo((FT + c) % 2, FT + c, min(PER_CHUNK, DOWN_TILES - c * PER_CHUNK) * P)

            def x_sum(base, ht, h):
                dve.wait_ge(group_done, count(base, ht, h))
                nc.vector.tensor_tensor(x_res[:, ht, half_of(h)], bank(base, ht, h),
                                        x_res[:, ht, half_of(h)], ALU.add).then_inc(x_summed, 1)

            def x_lo_part(base, ht, h):
                dve.wait_ge(x_hi, count(base, ht, h))
                dst = x3_hl if base == L2 else x_hl
                lo(dst[:, 1, ht, half_of(h)], x_res[:, ht, half_of(h)],
                   dst[:, 0, ht, half_of(h)]).then_inc(x_ready, 1)

            def late(name):
                dve.wait_ge(late_hi, LATE[name])

            def x_groups(base, which):
                for i, (ht, h) in enumerate(which):
                    x_sum(base, ht, h)
                    if i:
                        x_lo_part(base, *which[i - 1])
                x_lo_part(base, *which[-1])

            down_chunk_lo(2)
            b_block_add(B_BLOCKS - 1, 0)
            x_groups(DOWN, [(0, 0), (0, 1)])
            down_chunk_lo(3)
            x_groups(DOWN, [(1, 0), (1, 1)])
            down_chunk_lo(4)
            down_chunk_lo(5)
            x_groups(DOWN, [(2, 0), (2, 1)])
            late("l1_b")
            for k in range(KT):
                last = cols_lo(l1_b_cols[k], l1_b_raw[:, :, k, :])
            last.then_inc(late_ready, 1)
            late("l1_a")
            add_signed(l1_a_rows, l1_a_raw).then_inc(late_ready, 1)
            x_sum(DOWN, KT - 1, 0)
            late("l2_w")
            for k in range(KT):
                if k == 1:
                    x_lo_part(DOWN, KT - 1, 0)
                last = lo(l2_w_hl[:, k, 1, :], l2_w_raw[:, k, :], l2_w_hl[:, k, 0, :])
            last.then_inc(late_ready, 1)
            late("l2_a")
            lo(l2_a_cols[:, :, :, 64:128], l2_a_raw, l2_a_cols[:, :, :, 0:64]).then_inc(late_ready, 1)

            def low_add(event, h):
                dve.wait_ge(t_signed, event)
                dst = t_rows[:, PAIRS * PT + h * HALF:PAIRS * PT + (h + 1) * HALF].rearrange(
                    "p (a t) -> p a t", t=PT)
                src = banks[:, LOW_BANK, :].rearrange("p (a t) -> p a t", t=PT)
                for r in range(2):
                    at = slice(r * SEQ, (r + 1) * SEQ)
                    last = t_add(slice(64 * r, 64 * r + 64), dst[:, :, at], src[:, :, at], 1.0)
                last.then_inc(t_ready, 1)

            def l2_low_lo(event, h):
                dve.wait_ge(t_signed, event)
                for blk in range(2):
                    last = nc.vector.scalar_tensor_tensor(
                        out=l2_t(2, h, blk), in0=l2_low(32 * blk, blk), scalar=L2_SCALE,
                        in1=l2_t(blk, h, blk).bitcast(F32), op0=ALU.mult, op1=ALU.subtract)
                last.then_inc(t_ready, 1)

            low_add(4, 0)
            late("l2_b")
            add_signed(l2_b_rows, l2_b_raw).then_inc(late_ready, 1)
            x_groups(L1, [(ht, 0) for ht in range(KT)])
            x_groups(DOWN, [(3, 1)])
            l2_low_lo(5, 0)
            low_add(6, 1)
            x_groups(L1, [(ht, 1) for ht in range(KT)])
            for ht in range(KT):
                x_sum(L2, ht, 0)
                dve.wait_ge(late_hi, LATE["l2_b"] + 1 + ht)
                lo(l3_w_hl[:, ht, 1, :], l3_w_raw[:, ht, :], l3_w_hl[:, ht, 0, :]).then_inc(late_ready, 1)
                x_lo_part(L2, ht, 0)
                if ht == 1:
                    l2_low_lo(7, 1)
            for k in range(KT):
                dve.wait_ge(late_hi, LATE["l3_w"] + 1 + k)
                cols_lo(l3_a_cols[k], l3_a_raw[:, :, k, :]).then_inc(late_ready, 1)
            for ht in range(KT):
                x_sum(L2, ht, 1)
                dve.wait_ge(late_hi, LATE["l3_a"] + 1 + ht)
                add_signed(l3_b_rows[:, ht, :], l3_b_raw[:, ht, :]).then_inc(late_ready, 1)
                if ht == KT - 1:
                    low_add(8, 0)
                x_lo_part(L2, ht, 1)
            dve.wait_ge(bias_landed, 16)
            for h in range(2):
                for ht in range(KT):
                    if (ht, h) == (2, 0):
                        low_add(9, 1)
                    dve.wait_ge(group_done, count(L3, ht, h))
                    nc.vector.scalar_tensor_tensor(
                        out=x_res[:, ht, half_of(h)], in0=bank(L3, ht, h),
                        scalar=bias_col[:, ht:ht + 1], in1=x_res[:, ht, half_of(h)],
                        op0=ALU.add, op1=ALU.add).then_inc(x_summed, 1)

        @block.tensor
        def _(pe):
            def passes(dst, w_hi_tile, w_lo_tile, m_hi, m_lo, start, stop=False):
                nc.tensor.matmul(dst, w_hi_tile, m_hi, start=start, stop=False)
                nc.tensor.matmul(dst, w_hi_tile, m_lo, start=False, stop=False)
                return nc.tensor.matmul(dst, w_lo_tile, m_hi, start=False, stop=stop)

            def x_tile(k, h, s, x=x_hl):
                return x[:, s, k, half_of(h)]

            def gate_up_k(slot, k, h):
                for w in range(2):
                    at = slice((2 * k + w) * P, (2 * k + w + 1) * P)
                    passes(banks[:, 2 * h + w, :], w_hl[:, slot, 0, at], w_hl[:, slot, 1, at],
                           x_tile(k, h, 0), x_tile(k, h, 1), k == 0, k == KT - 1)

            def gate_up_low(slot, h):
                for w in range(2):
                    for pair in range(2 * h, 2 * h + 2):
                        c0 = (pair % 2) * PT
                        last = nc.tensor.matmul(banks[:, 2 * h + w, c0:c0 + PT],
                                                b_rows[:, slot, pair, w * P:(w + 1) * P],
                                                t_rows[:, (2 * pair + w) * PT:(2 * pair + w + 1) * PT],
                                                start=False, stop=True, skip_group_check=True)
                last.then_inc(gate_up_done, 1)

            def down_low(act_of, slot):
                for pair in range(PAIRS):
                    for s in range(2):
                        last = nc.tensor.matmul(banks[:, 4 + pair, 0:PT], down_a_cols[:, slot, pair, :],
                                                act_of(s, pair), start=False, stop=True,
                                                skip_group_check=True)
                return last

            def gu_low_cols(h):
                for pair in range(2 * h, 2 * h + 2):
                    for w in range(2):
                        for k in range(KT):
                            for s in range(2):
                                last = nc.tensor.matmul(
                                    banks[:, 4 + pair, w * PT:(w + 1) * PT],
                                    gu_a_cols[:, w, k, pair * P:(pair + 1) * P],
                                    x_hl[:, s, k, pair_of(pair)], start=(k == 0 and s == 0),
                                    stop=(k == KT - 1 and s == 1))
                last.then_inc(low_done, 1)

            pe.wait_ge(zeros_set, 1)
            for _ in range(18):
                nc.tensor.matmul(banks[:, 7, 0:PT], zeros[:, 0:P], zeros[:, :], start=True, stop=True)
            for c in range(KT + 2):
                pe.wait_ge(piece_ready, c + 1)
                gate_up_k(0, c % KT, c // KT)
            pe.wait_ge(gu_a_ready, 1)
            gu_low_cols(0)
            pe.wait_ge(piece_ready, 2 * KT)
            gu_low_cols(1)
            pe.wait_ge(t_ready, 1)
            pe.wait_ge(b_ready, 1)
            gate_up_low(0, 0)
            for k in range(2, KT):
                gate_up_k(0, k, 1)
            pe.wait_ge(t_ready, 2)
            gate_up_low(0, 1)
            for pair in range(PAIRS):
                nc.tensor.matmul(banks[:, 4 + pair, 0:PT], zeros[:, 0:P], zeros[:, :], start=True, stop=True)

            with nc.Fori(0, (FT - 1) // 2, engines=[PE_ENGINE]) as i:
                for u in range(2):
                    ft, slot = 2 * i + (1 + u), (1 + u) % 2
                    pe.wait_ge(w_ready, ft)
                    for h in range(2):
                        pe.wait_ge(product_done, 2 * ft + (h - 1))
                        for k in range(KT):
                            gate_up_k(slot, k, h)
                        if h == 0:
                            pe.wait_ge(b_ready, ft + 1)
                        gate_up_low(slot, h)
                        if h == 0:
                            pe.wait_ge(down_a_ready, ft)
                            pe.wait_ge(act_ready, 2 * ft)
                            prev = bass.ds(ft - 1, 1)
                            down_low(lambda s, pair: act_hl[:, prev, s, pair_of(pair)].rearrange(
                                "p a t -> p (a t)"), 1 - slot)

            def down_tile(t, halves, freed=None):
                ht, k = divmod(t, FT)
                c, at = divmod(t, PER_CHUNK)
                slot = (FT + c) % 2
                cols = slice(at * P, (at + 1) * P)
                if at == 0:
                    pe.wait_ge(w_ready, FT + c)
                for h in halves:
                    if k == 0 and ht < 2:
                        pe.wait_ge(product_done, 2 * FT - 1 + ht)
                    elif k == 0 and bank_free(DOWN, ht, h):
                        pe.wait_ge(x_summed, bank_free(DOWN, ht, h))
                    last = passes(bank(DOWN, ht, h), w_hl[:, slot, 0, cols], w_hl[:, slot, 1, cols],
                                  act_hl[:, k, 0, half_of(h)], act_hl[:, k, 1, half_of(h)], k == 0,
                                  k == FT - 1)
                if freed is not None:
                    last.then_inc(freed, 1)

            def low_rows(base, ht, h, rows_of, t_base):
                for pair in range(2 * h, 2 * h + 2):
                    c0 = (pair % 2) * PT
                    last = nc.tensor.matmul(bank(base, ht, h)[:, c0:c0 + PT], rows_of(pair),
                                            t_rows[:, t_base + pair * PT:t_base + (pair + 1) * PT],
                                            start=(base == L1 and pair % 2 == 0), stop=True,
                                            skip_group_check=True)
                last.then_inc(group_done, 1)

            def down_rows(ht, h):
                low_rows(DOWN, ht, h, lambda pair: b_rows[
                    :, (FT + ht // 2) % 2, pair, (ht % 2) * P:(ht % 2 + 1) * P], 0)

            for ht in range(KT - 1):
                for k in range(FT):
                    t = ht * FT + k
                    if t == 3:
                        pe.wait_ge(act_ready, 2 * FT)
                        pe.wait_ge(down_a_ready, FT)
                        down_low(lambda s, pair: act_hl[:, FT - 1, s, pair_of(pair)],
                                 (FT - 1) % 2).then_inc(low_done, 1)
                    down_tile(t, range(2), down_chunk_used if t % PER_CHUNK == PER_CHUNK - 1 else None)
                if ht == 0:
                    pe.wait_ge(t_ready, 3)
                    pe.wait_ge(b_ready, FT + 1)
                elif ht == 2:
                    pe.wait_ge(b_ready, B_BLOCKS)
                for h in range(2):
                    down_rows(ht, h)
            def low_cols(cols, h, x):
                for pair in range(2 * h, 2 * h + 2):
                    c0 = (pair % 2) * PT
                    for k in range(KT):
                        for s in range(2):
                            last = nc.tensor.matmul(banks[:, LOW_BANK, c0:c0 + PT],
                                                    cols[k][:, pair * P:(pair + 1) * P],
                                                    x[:, s, k, pair_of(pair)],
                                                    start=(k == 0 and s == 0),
                                                    stop=(k == KT - 1 and s == 1))
                last.then_inc(low_done, 1)

            def l1_groups(event, h):
                pe.wait_ge(t_ready, event)
                for ht in range(KT):
                    pe.wait_ge(x_summed, bank_free(L1, ht, h))
                    low_rows(L1, ht, h, lambda pair: l1_a_rows[:, pair, ht * P:(ht + 1) * P], PAIRS * PT)

            for k in range(FT):
                down_tile((KT - 1) * FT + k, [0], act_tile_used)
            down_rows(KT - 1, 0)
            for k in range(FT):
                if k == 4:
                    pe.wait_ge(late_ready, LATE["l1_b"])
                    pe.wait_ge(x_ready, count(DOWN, KT - 1, 0))
                    low_cols(l1_b_cols, 0, x_hl)
                if k == 7:
                    pe.wait_ge(late_ready, LATE["l1_a"])
                    l1_groups(4, 0)
                down_tile((KT - 1) * FT + k, [1], act_tile_used)
            down_rows(KT - 1, 1)

            def main(base, ht, h, w, x, tiles=range(KT)):
                cols = slice(ht * P, (ht + 1) * P)
                if tiles[0] == 0 and bank_free(base, ht, h):
                    pe.wait_ge(x_summed, bank_free(base, ht, h))
                for k in tiles:
                    passes(bank(base, ht, h), w[:, k, 0, cols], w[:, k, 1, cols],
                           x_tile(k, h, 0, x), x_tile(k, h, 1, x), k == 0, k == KT - 1)

            def l2_low_cols(h, tiles=range(KT)):
                for k in tiles:
                    pe.wait_ge(x_ready, count(L1, k, h))
                    for pair in range(2 * h, 2 * h + 2):
                        for s in range(2):
                            last = nc.tensor.matmul(
                                banks[:, L2_LOW_BANK, (pair % 2) * PT:(pair % 2 + 1) * PT],
                                l2_a_cols[:, k, pair, :], x_hl[:, s, k, pair_of(pair)],
                                start=(k == 0 and pair % 2 == 0 and s == 0), stop=True,
                                skip_group_check=True)
                if k == KT - 1:
                    last.then_inc(low_done, 1)

            def l2_main(ht, h, tiles=range(KT)):
                main(L2, ht, h, l2_w_hl, x_hl, tiles)

            def l2_rows(ht, h):
                pe.wait_ge(t_ready, 5 + 2 * h)
                nc.tensor.matmul(bank(L2, ht, h), l2_b_rows[:, ht * P:(ht + 1) * P],
                                 t_rows[:, half_of(h)], start=False, stop=True,
                                 skip_group_check=True).then_inc(group_done, 1)

            def l3_group(ht, h):
                main(L3, ht, h, l3_w_hl, x3_hl)
                pe.wait_ge(late_ready, LATE["l3_b"])
                pe.wait_ge(t_ready, 8 + h)
                low_rows(L3, ht, h, lambda pair: l3_b_rows[:, pair, ht * P:(ht + 1) * P], PAIRS * PT)

            pe.wait_ge(late_ready, LATE["l2_a"])
            for k in range(KT):
                l2_low_cols(0, [k])
                l2_main(0, 0, [k])
                if k == 0:
                    l2_main(1, 0, [k])
            pe.wait_ge(x_ready, count(DOWN, KT - 1, 1))
            low_cols(l1_b_cols, 1, x_hl)
            l2_main(1, 0, range(1, KT))
            l1_groups(6, 1)
            pe.wait_ge(late_ready, LATE["l2_b"])
            l2_rows(0, 0)
            l2_rows(1, 0)
            l2_main(2, 0)
            l2_rows(2, 0)
            l2_main(3, 0)
            l2_low_cols(1)
            l2_rows(3, 0)
            l2_main(0, 1)
            l2_main(1, 1)
            l2_rows(0, 1)
            l2_rows(1, 1)
            l2_main(2, 1)
            l2_rows(2, 1)
            l2_main(KT - 1, 1)
            l2_rows(KT - 1, 1)
            pe.wait_ge(late_ready, LATE["l3_a"])
            pe.wait_ge(x_ready, count(L2, KT - 1, 0))
            low_cols(l3_a_cols, 0, x3_hl)
            for ht in range(KT):
                l3_group(ht, 0)
                if ht == 1:
                    pe.wait_ge(x_ready, count(L2, KT - 1, 1))
                    low_cols(l3_a_cols, 1, x3_hl)
            for ht in range(KT):
                l3_group(ht, 1)


def kernel(**inputs):
    import numpy as np
    import concourse.bacc as bacc
    from concourse.bass_utils import run_bass_kernel_spmd

    a = {k: np.asarray(v) for k, v in inputs.items()}

    def pad_f(m, axis):
        widths = [(0, 0)] * m.ndim
        widths[axis] = (0, FPAD - FFN)
        return np.pad(m, widths)

    def cols_table(t):
        n, r, f = t.shape
        return t.reshape(n, r, f // P, P).transpose(0, 3, 2, 1)

    def gate_up_tiles(w):
        return pad_f(w, 0).reshape(FT, P, KT, P).transpose(0, 3, 2, 1)

    gu = np.stack([gate_up_tiles(a["L0_cond_W_gate"]), gate_up_tiles(a["L0_cond_W_up"])], 3)
    gu = gu.reshape(FT, P, CHUNK)
    down = pad_f(a["L0_cond_W_down"], 1).reshape(KT, P, FT, P).transpose(0, 2, 3, 1)
    down = np.pad(down.reshape(DOWN_TILES, P, P),
                  [(0, DOWN_CHUNKS * PER_CHUNK - DOWN_TILES), (0, 0), (0, 0)])
    down = down.reshape(DOWN_CHUNKS, PER_CHUNK, P, P).transpose(0, 2, 1, 3).reshape(DOWN_CHUNKS, P, CHUNK)

    def rows_ffn(t):
        return pad_f(t[0], 1).reshape(-1, FT, P, RANK).transpose(0, 1, 3, 2)

    up_b = np.stack([rows_ffn(a["L0_cond_B_gate"]), rows_ffn(a["L0_cond_B_up"])], 3)
    up_b = up_b.reshape(-1, FT, RANK, 2 * P)
    down_b = a["L0_cond_B_down"][0].reshape(-1, KT // 2, 2 * P, RANK).transpose(0, 1, 3, 2)

    def square(w):
        return w.T.reshape(KT, P, HID).transpose(1, 0, 2).reshape(P, KT * HID)

    sign = np.zeros((P, 3), np.float32)
    sign[2::4, 0] = -1.0
    sign[1::4, 1] = -1.0
    sign[P // 4:P // 2, 2] = -1.0
    data = {
        "x_t": a["x"].reshape(TOK, HID).T.reshape(KT, P, TOK),
        "weights": np.concatenate([gu, down], 0),
        "indices": np.concatenate([a["itok_B_2_6"], a["itok_B_3_7"], a["itok_B_0_2"],
                                   a["itok_B_6_15"]]).reshape(1, 4 * BATCH),
        "gu_a": np.stack([cols_table(a["L0_cond_A_gate"][0]), cols_table(a["L0_cond_A_up"][0])],
                         2).reshape(ADAPTERS["l0"], P, 2 * KT * RANK),
        "up_b": np.concatenate([up_b, down_b], 1),
        "down_a": cols_table(pad_f(a["L0_cond_A_down"][0], 2)).reshape(ADAPTERS["l0"], P, FT * RANK),
        "l1_b": cols_table(a["L1_cond_B"]).reshape(ADAPTERS["l1"], P, KT * RANK),
        "l1_a": a["L1_cond_A"].transpose(0, 2, 1),
        "l2_w": square(a["L2_cond_W"]),
        "l2_a": cols_table(a["L2_cond_lora_A"].transpose(0, 2, 1)),
        "l2_b": np.tile(a["L2_cond_lora_B_w"].T, (COPIES, 1)),
        "l3_w": square(a["L3_cond_base_weight"]),
        "l3_a": cols_table(a["L3_cond_lora_A_w"]).reshape(ADAPTERS["l3"], P, KT * RANK),
        "l3_b": a["L3_cond_lora_B_w"].transpose(0, 2, 1),
        "bias": a["L3_cond_base_bias"].reshape(KT, P).T,
        "row_signs": sign,
    }
    nc = bacc.Bacc("TRN2", target_bir_lowering=False, num_devices=1)
    arrays, args = {}, []
    for name, v in data.items():
        arrays[name] = np.ascontiguousarray(v)
        args.append(nc.dram_tensor(name, v.shape, mybir.dt.from_np(v.dtype), kind="ExternalInput").ap())
    out_t = nc.dram_tensor("out_t", (KT, P, TOK), F32, kind="ExternalOutput").ap()
    lora_chain_kernel(nc, *args, out_t)
    r = run_bass_kernel_spmd(nc, [arrays], core_ids=[0])
    got = r.results[0]["out_t"]
    return np.ascontiguousarray(got.reshape(HID, TOK).T).reshape(BATCH, SEQ, HID)
```

```python
from contextlib import ExitStack

import concourse.bass as bass
from concourse import mybir

F32 = mybir.dt.float32
F32R = mybir.dt.float32r
ALU = mybir.AluOpType
ACT = mybir.ActivationFunctionType
DVE_ENGINE = mybir.EngineType.DVE
ACT_ENGINE = mybir.EngineType.Activation
PE_ENGINE = mybir.EngineType.PE
SP_ENGINE = mybir.EngineType.SP
POOL_ENGINE = mybir.EngineType.Pool

P = 128
BATCH, SEQ, HID, FFN = 8, 128, 512, 1376
TOK = BATCH * SEQ
KT = HID // P
FT = -(-FFN // P)
FPAD = FT * P
HALF = TOK // 2
PAIRS = BATCH // 2
PT = 2 * SEQ
RANK = 16
COPIES = 4
DOWN_TILES = KT * FT
PER_CHUNK = 8
CHUNK = PER_CHUNK * P
DOWN_CHUNKS = -(-DOWN_TILES // PER_CHUNK)
CHUNKS = FT + DOWN_CHUNKS
B_BLOCKS = FT + KT // 2
L0_SCALE, L2_SCALE = 0.5, 0.5
ADAPTERS = {"l0": 16, "l1": 8, "l2": 5, "l3": 32}


def lora_chain_kernel(nc, x_t, weights, indices, gu_a, up_b, down_a, l1_b, l1_a, l2_w, l2_a, l2_b,
                      l3_w, l3_a, l3_b, bias, row_signs, out):
    ctx = ExitStack()
    with ctx:
        def sb(name, shape, dt=F32):
            return ctx.enter_context(nc.sbuf_tensor(name, shape, dt))

        def sem(name):
            return ctx.enter_context(nc.semaphore(name))

        act_hl = sb("act_hl", [P, FT, 2, TOK], F32R)
        x_hl = sb("x_hl", [P, 2, KT, TOK], F32R)
        w_hl = sb("w_hl", [P, 2, 2, CHUNK], F32R)
        b_rows = sb("b_rows", [P, 2, PAIRS, 2 * P], F32R)
        down_a_cols = sb("down_a_cols", [P, 2, PAIRS, P], F32R)
        t_rows = sb("t_rows", [P, 2 * PAIRS * PT], F32R)
        zeros = sb("zeros", [P, PT], F32R)

        def freed(tile, n, h):
            return act_hl[:, tile:tile + n, :, h * HALF:(h + 1) * HALF].rearrange("p a s t -> p (a s) t")

        gu_a_cols = act_hl[:, 9:11, :, :].rearrange("p a b c -> p (a b c)").rearrange(
            "p (w k c) -> p w k c", w=2, k=KT)
        l1_b_cols = [down_a_cols[:, k, :, :].rearrange("p a c -> p (a c)") for k in range(2)] + [
            freed(0, 1, 0)[:, s, :] for s in range(2)]
        l1_a_rows = freed(1, 2, 0)
        l2_w_hl = act_hl[:, 3:3 + KT, :, 0:HALF]
        l2_a_cols = act_hl[:, 0:KT, 0, HALF:TOK].rearrange("p k (a c) -> p k a c", a=PAIRS)
        l2_b_rows = act_hl[:, 4, 0, HALF:TOK]
        l3_b_rows = l1_a_rows
        x3_hl = act_hl[:, 7:7 + KT, :, :].rearrange("p k s t -> p s k t")
        l3_w_hl = w_hl[:, :, :, :].rearrange("p a b c -> p (a b c)").rearrange(
            "p (k s o) -> p k s o", s=2, k=KT)
        l3_a_cols = b_rows[:, :, :, :].rearrange("p a b c -> p (a b c)").rearrange(
            "p (k c) -> p k c", k=KT)
        l3_a_cols = [l3_a_cols[:, k, :] for k in range(KT)]

        x_res = sb("x_res", [P, KT, TOK])
        w_raw = sb("w_raw", [P, 2, CHUNK])
        b_raw = sb("b_raw", [P, PAIRS, 2 * P])
        down_a_raw = sb("down_a_raw", [P, BATCH, FT, RANK])
        low_raw = sb("low_raw", [P, 4 * HID])
        silu_out = sb("silu_out", [P, 4 * HID])
        bias_col = sb("bias_col", [P, KT])
        sign_col = sb("sign_col", [P, 3])
        t_sign, b_sign = sign_col[:, 0:1], sign_col[:, 1:2]
        t_sign_half = sb("t_sign_half", [P, 1])
        scratch = sb("scratch", [P, 1])

        down_a_flat = down_a_raw[:, :, :, :].rearrange("p a b c -> p (a b c)")
        gu_a_raw = low_raw[:, 0:1024].rearrange("p (b w k r) -> p b w k r", b=BATCH, w=2, k=KT)
        l1_b_raw = down_a_flat[:, 0:512].rearrange("p (b k r) -> p b k r", b=BATCH, k=KT)
        l2_b_raw = down_a_flat[:, 512:1024]
        l1_a_raw = low_raw[:, :].rearrange("p (r o) -> p r o", r=PAIRS)
        b_raw_at = [b_raw[:, :, :], silu_out[:, 2 * HID:].rearrange("p (a c) -> p a c", a=PAIRS)]
        l2_w_raw = silu_out[:, :].rearrange("p (k o) -> p k o", k=KT)
        l2_a_raw = b_raw[:, :, :].rearrange("p a b -> p (a b)").rearrange(
            "p (k a c) -> p k a c", k=KT, a=PAIRS)
        l3_w_raw = w_raw[:, :, :].rearrange("p a b -> p (a b)").rearrange("p (k o) -> p k o", k=KT)
        l3_a_raw = l1_b_raw
        l3_b_raw = l1_a_raw

        banks = ctx.enter_context(nc.psum_tensor("banks", [P, 8, 512], F32))

        w_piece_landed = [sem(f"w_piece_landed{k}") for k in range(KT)]
        x_piece_landed = [sem(f"x_piece_landed{c}") for c in range(2 * KT)]
        signs_landed = sem("signs_landed")
        bias_landed = sem("bias_landed")
        w_piece_hi = sem("w_piece_hi")
        w_piece_ready = sem("w_piece_ready")
        x_piece_hi = sem("x_piece_hi")
        piece_ready = sem("piece_ready")
        w_landed = [sem(f"w_landed{s}") for s in range(2)]
        w_hi = sem("w_hi")
        w_ready = sem("w_ready")
        b_landed = [sem(f"b_landed{s}") for s in range(2)]
        b_by_pool_landed = sem("b_by_pool_landed")
        b_signed = sem("b_signed")
        b_ready = sem("b_ready")
        gu_a_landed = [sem(f"gu_a_landed{s}") for s in range(2)]
        gu_a_hi = sem("gu_a_hi")
        gu_a_ready = sem("gu_a_ready")
        down_a_landed = sem("down_a_landed")
        down_a_hi = sem("down_a_hi")
        down_a_ready = sem("down_a_ready")
        scratch_zeroed = sem("scratch_zeroed")
        zeros_set = sem("zeros_set")
        t_zeroed = sem("t_zeroed")
        sign_scaled = sem("sign_scaled")
        low_done = sem("low_done")
        t_half_signed = sem("t_half_signed")
        t_ready = sem("t_ready")
        gate_up_done = sem("gate_up_done")
        silu_done = sem("silu_done")
        product_done = sem("product_done")
        act_hi = sem("act_hi")
        act_ready = sem("act_ready")
        down_chunk_used = sem("down_chunk_used")
        act_tile_used = sem("act_tile_used")
        group_done = sem("group_done")
        x_summed = sem("x_summed")
        x_hi = sem("x_hi")
        x_ready = sem("x_ready")
        late_landed = {n: sem(f"{n}_landed") for n in
                       ("l2_w", "l1_b", "l1_a", "l2_a", "l2_b", "l3_w", "l3_a", "l3_b")}
        late_hi = sem("late_hi")
        late_ready = sem("late_ready")
        out_stored = sem("out_stored")
        LATE = {"l1_b": 1, "l1_a": 2, "l2_w": 3, "l2_a": 4, "l2_b": 5, "l3_w": 5 + KT,
                "l3_a": 5 + 2 * KT, "l3_b": 5 + 2 * KT + PAIRS}
        LOW_GATE_UP = range(1, 1 + PAIRS)
        LOW_DOWN = PAIRS + 1
        LOW_L1, LOW_L2, LOW_L3 = [[PAIRS + 2 + n for n in both] for both in ((0, 2), (1, 3), (4, 5))]
        DOWN, L1, L2, L3 = range(4)
        ORDER = [(DOWN, ht, h) for ht in range(KT - 1) for h in range(2)] + [(DOWN, KT - 1, 0)] + \
            [(L1, ht, 0) for ht in range(KT)] + [(DOWN, KT - 1, 1)] + [(L1, ht, 1) for ht in range(KT)] + \
            [(layer, ht, h) for layer in (L2, L3) for h in range(2) for ht in range(KT)]
        BANKS = [0, 1, 2, 3, 4, 0, 1] + [3, 4, 0, 1] + [2] + [4, 0, 1, 2] + [7, 3, 4, 0, 1, 2, 7, 3] + \
            [4, 0, 1, 2, 7, 3, 4, 0]
        PLACE = {g: n for n, g in enumerate(ORDER)}
        GU_A_BY_POOL = BATCH // 2
        GU_A_BY_ACT = {c: [GU_A_BY_POOL + c] for c in range(BATCH - GU_A_BY_POOL)}
        B_BY_POOL = BATCH // 2
        B_BY_ACT = {4: [4, 5], 5: [6, 7]}
        PIECES_BEFORE_A = 6
        LOW_BANK, L2_LOW_BANK = 5, 6

        def count(layer, ht, h):
            return PLACE[(layer, ht, h)] + 1

        def bank(layer, ht, h):
            return banks[:, BANKS[PLACE[(layer, ht, h)]], :]

        def bank_free(layer, ht, h):
            n = PLACE[(layer, ht, h)]
            return max([m + 1 for m in range(n) if BANKS[m] == BANKS[n]], default=0)

        def half_of(h):
            return slice(h * HALF, (h + 1) * HALF)

        def pair_of(pair):
            return slice(pair * PT, (pair + 1) * PT)

        def cols_view(cols):
            v = cols.rearrange("p (b r g) -> p b r g", r=RANK, g=COPIES)
            return v[:, :, :, 0:3], v[:, :, :, 3]

        def gate_up_values(pair):
            return (banks[:, 4 + pair, :].rearrange("p (w t) -> p w t", w=2),
                    t_rows[:, 2 * pair * PT:(2 * pair + 2) * PT].rearrange("p (w t) -> p w t", w=2))

        def l2_t(quarter, h, blk):
            return t_rows[32 * quarter:32 * quarter + 32, half_of(h)].rearrange(
                "p (a t) -> p a t", t=PT)[:, :, blk * SEQ:(blk + 1) * SEQ]

        def l2_low(row, blk):
            return banks[row:row + 32, L2_LOW_BANK, :].rearrange(
                "p (a t) -> p a t", t=PT)[:, :, blk * SEQ:(blk + 1) * SEQ]

        OUT_PARTS = [(ht, half_of(h)) for h in range(2) for ht in range(KT)][:-1] + \
            [(KT - 1, pair_of(pair)) for pair in (PAIRS - 2, PAIRS - 1)]
        FIRST_OUT = count(L3, 0, 0)

        def out_bank(ht, tokens):
            return banks[:, L2_LOW_BANK, :] if (ht, tokens) == OUT_PARTS[-1] else \
                bank(L3, ht, tokens.start // HALF)

        block = ctx.enter_context(nc.Block())

        def load_adapters(eng, engine_type, layer, name):
            at = layer * BATCH
            return nc.values_load_multi_w_load_instructions(
                indices[0:1, at:at + BATCH], engines=[engine_type], min_val=0,
                max_val=ADAPTERS[name] - 1)[1]

        def gather_rows(eng, table, adapter, raw, landed, batches=range(BATCH)):
            for b in batches:
                src = table(adapter[b])
                rows = slice(64 * (b % 2), 64 * (b % 2) + 64)
                eng.dma_start(raw[rows, b // 2, :], src.unsqueeze(1).broadcast_to(
                    [RANK, COPIES, src.shape[-1]])).then_inc(landed, 16)

        def gather_cols(table, adapter, raw_of, landed, eng, batches=range(BATCH)):
            for b in batches:
                src = table[bass.ds(adapter[b], 1)]
                src = src.rearrange("a p k r -> (a p) k r") if len(src.shape) == 4 else \
                    src.rearrange("a p c -> (a p) c")
                eng.dma_start(raw_of(b), src).then_inc(landed, 16)

        def b_block(n):
            return lambda a: up_b[bass.ds(a, 1), n].rearrange("a r c -> (a r) c")

        def gu_a_raw_of(b):
            return gu_a_raw[:, b, :, :, :].rearrange("p w k r -> p (w k r)")

        @block.sync
        def _(sp):
            def x_piece(c):
                h, k = divmod(c, KT)
                sp.dma_start(x_res[:, k, half_of(h)], x_t[k, :, half_of(h)]).then_inc(x_piece_landed[c], 16)

            for k in range(KT):
                sp.dma_start(w_raw[:, 0, k * 256:(k + 1) * 256],
                             weights[0, :, k * 256:(k + 1) * 256]).then_inc(w_piece_landed[k], 16)
                x_piece(k)
            for c in range(KT, 2 * KT):
                x_piece(c)
            sp.dma_start(sign_col[:, :], row_signs).then_inc(signs_landed, 16)
            sp.dma_start(w_raw[:, 1, :], weights[1]).then_inc(w_landed[1], 16)
            l0 = load_adapters(sp, SP_ENGINE, 0, "l0")
            gather_rows(sp, b_block(1), l0, b_raw_at[1], b_landed[1])
            sp.wait_ge(piece_ready, KT)
            sp.dma_start(w_raw[:, 0, :], weights[2]).then_inc(w_landed[0], 16)
            with nc.Fori(0, (FT - 1) // 2, engines=[SP_ENGINE]) as i:
                for u in range(2):
                    sp.wait_ge(b_ready, 2 * i + (1 + u))
                    gather_rows(sp, lambda a: up_b[bass.ds(a, 1), bass.ds(2 * i + (2 + u), 1)].rearrange(
                        "a n r c -> (a n r) c"), l0, b_raw_at[u], b_landed[u])
                    sp.wait_ge(w_ready, 2 * i + (1 + u))
                    sp.dma_start(w_raw[:, (1 + u) % 2, :], weights[bass.ds(2 * i + (3 + u), 1)].rearrange(
                        "a p c -> (a p) c")).then_inc(w_landed[(1 + u) % 2], 16)
            sp.wait_ge(b_ready, B_BLOCKS - 2)
            gather_rows(sp, b_block(B_BLOCKS - 1), l0, b_raw_at[0], b_landed[0])
            for n in range(FT + 2, CHUNKS):
                sp.wait_ge(w_ready, n - 2)
                sp.dma_start(w_raw[:, n % 2, :], weights[n]).then_inc(w_landed[n % 2], 16)
                if n == FT + 2:
                    sp.wait_ge(act_ready, 2 * FT)
                    sp.wait_ge(b_ready, B_BLOCKS - 1)
                    sp.dma_start(silu_out[:, :], l2_w).then_inc(late_landed["l2_w"], 16)
                    sp.wait_ge(down_a_ready, FT)
                    sp.dma_start(l2_b_raw, l2_b).then_inc(late_landed["l2_b"], 16)
            sp.wait_ge(w_ready, CHUNKS - 1)
            sp.dma_start(w_raw[:, :, :].rearrange("p a b -> p (a b)"), l3_w).then_inc(
                late_landed["l3_w"], 16)
            for n, (ht, tokens) in enumerate(OUT_PARTS):
                sp.wait_ge(x_summed, FIRST_OUT + n)
                sp.dma_start(out[ht, :, tokens], x_res[:, ht, tokens]).then_inc(out_stored, 16)
            sp.wait_ge(out_stored, 16 * len(OUT_PARTS))

        @block.gpsimd
        def _(pool):
            l0 = load_adapters(pool, POOL_ENGINE, 0, "l0")
            gather_cols(gu_a, l0, gu_a_raw_of, gu_a_landed[0], pool, range(GU_A_BY_POOL))
            gather_rows(pool, b_block(0), l0, b_raw_at[0], b_by_pool_landed, range(B_BY_POOL))
            pool.dma_start(bias_col[:, :], bias).then_inc(bias_landed, 16)
            gather_cols(down_a, l0, lambda b: down_a_raw[:, b, :, :].rearrange(
                "p f r -> p (f r)"), down_a_landed, pool)
            l1 = load_adapters(pool, POOL_ENGINE, 1, "l1")
            pool.wait_ge(gu_a_ready, 2 * KT)
            gather_rows(pool, lambda a: l1_a[bass.ds(a, 1)].rearrange("a r o -> (a r) o"), l1, l1_a_raw,
                        late_landed["l1_a"])
            pool.wait_ge(down_a_ready, FT)
            gather_cols(l1_b, l1, lambda b: l1_b_raw[:, b, :, :].rearrange("p k r -> p (k r)"),
                        late_landed["l1_b"], pool)
            l2 = load_adapters(pool, POOL_ENGINE, 2, "l2")
            pool.wait_ge(b_ready, B_BLOCKS)
            gather_cols(l2_a, l2, lambda b: l2_a_raw[:, :, b // 2, 32 * (b % 2):32 * (b % 2) + 32],
                        late_landed["l2_a"], pool)
            l3 = load_adapters(pool, POOL_ENGINE, 3, "l3")
            pool.wait_ge(late_ready, LATE["l1_b"])
            gather_cols(l3_a, l3, lambda b: l3_a_raw[:, b, :, :].rearrange("p k r -> p (k r)"),
                        late_landed["l3_a"], pool)
            pool.wait_ge(late_ready, LATE["l1_a"])
            gather_rows(pool, lambda a: l3_b[bass.ds(a, 1)].rearrange("a r o -> (a r) o"), l3, l3_b_raw,
                        late_landed["l3_b"])

        @block.scalar
        def _(act):
            def hi(dst, src):
                return nc.scalar.activation(dst, src, ACT.Copy)

            def signed(dst, src, sign):
                return nc.scalar.activation(dst, src, ACT.Copy, scale=sign)

            act.wait_ge(scratch_zeroed, 1)
            nc.scalar.activation(scratch[:, :], scratch[:, :], ACT.Silu)
            l0 = load_adapters(act, ACT_ENGINE, 0, "l0")
            for c in range(2 * KT):
                h, k = divmod(c, KT)
                if c == PIECES_BEFORE_A:
                    act.wait_ge(gu_a_landed[0], 16 * GU_A_BY_POOL)
                    act.wait_ge(gu_a_landed[1], 16 * (BATCH - GU_A_BY_POOL))
                    for n in range(2 * KT):
                        his, _ = cols_view(gu_a_cols[:, n // KT, n % KT, :])
                        hi(his, gu_a_raw[:, :, n // KT, n % KT, :].unsqueeze(3).broadcast_to(
                            [P, BATCH, RANK, 3])).then_inc(gu_a_hi, 1)
                if h == 0:
                    act.wait_ge(w_piece_landed[k], 16)
                    hi(w_hl[:, 0, 0, k * 256:(k + 1) * 256], w_raw[:, 0, k * 256:(k + 1) * 256]).then_inc(
                        w_piece_hi, 1)
                act.wait_ge(x_piece_landed[c], 16)
                hi(x_hl[:, 0, k, half_of(h)], x_res[:, k, half_of(h)]).then_inc(x_piece_hi, 1)
                gather_cols(gu_a, l0, gu_a_raw_of, gu_a_landed[1], act, GU_A_BY_ACT.get(c, []))
                gather_rows(act, b_block(0), l0, b_raw_at[0], b_landed[0], B_BY_ACT.get(c, []))

            def b_elsewhere(slot):
                return 16 * B_BY_POOL if slot == 0 else 0

            def b_block_signed(slot, landed):
                act.wait_ge(b_landed[slot], landed - b_elsewhere(slot))
                signed(b_rows[:, slot, :, :], b_raw_at[slot], b_sign).then_inc(b_signed, 1)

            def t_split(row_half, dst, src, sign):
                rows = slice(64 * row_half, 64 * row_half + 64)
                return signed(dst[rows], src[rows], sign[rows])

            def weights_hi(slot, landed):
                act.wait_ge(w_landed[slot], landed)
                hi(w_hl[:, slot, 0, :], w_raw[:, slot, :]).then_inc(w_hi, 1)

            act.wait_ge(signs_landed, 16)
            act.wait_ge(b_by_pool_landed, 16 * B_BY_POOL)
            b_block_signed(0, 16 * BATCH)
            weights_hi(1, 16)
            act.wait_ge(t_zeroed, 1)
            act.wait_ge(sign_scaled, 1)
            for pair in range(PAIRS):
                act.wait_ge(low_done, LOW_GATE_UP[pair])
                gu_low, gu_t = gate_up_values(pair)
                for r in range(2):
                    at = slice(r * SEQ, (r + 1) * SEQ)
                    t_split(r, gu_t[:, :, at], gu_low[:, :, at], t_sign_half).then_inc(t_half_signed, 1)
            act.wait_ge(down_a_landed, 16 * BATCH)
            for h in range(2):
                act.wait_ge(gate_up_done, h + 1)
                nc.scalar.activation(silu_out[:, half_of(h)], banks[:, 2 * h, :], ACT.Silu).then_inc(
                    silu_done, 1)
                if h == 1:
                    b_block_signed(1, 16 * BATCH)
                    his, _ = cols_view(down_a_cols[:, 0, :, :].rearrange("p a c -> p (a c)"))
                    hi(his, down_a_raw[:, :, 0, :].unsqueeze(3).broadcast_to(
                        [P, BATCH, RANK, 3])).then_inc(down_a_hi, 1)
                act.wait_ge(product_done, h + 1)
                hi(act_hl[:, 0, 0, half_of(h)], silu_out[:, half_of(h)]).then_inc(act_hi, 1)
            with nc.Fori(0, (FT - 1) // 2, engines=[ACT_ENGINE]) as i:
                for u in range(2):
                    ft, slot = 2 * i + (1 + u), (1 + u) % 2
                    ft_at = bass.ds(ft, 1)

                    def act_at(h):
                        return act_hl[:, ft_at, 0, half_of(h)].rearrange("p a t -> p (a t)")

                    for h in range(2):
                        step = 4 * i + (2 + 2 * u + h)
                        act.wait_ge(gate_up_done, step + 1)
                        act.wait_ge(act_ready, step - 1)
                        nc.scalar.activation(silu_out[:, half_of(h)], banks[:, 2 * h, :],
                                             ACT.Silu).then_inc(silu_done, 1)
                        if h == 0:
                            act.wait_ge(w_landed[1 - slot], 16 * i + 16 * (1 + u))
                            hi(w_hl[:, 1 - slot, 0, :], w_raw[:, 1 - slot, :]).then_inc(w_hi, 1)
                        else:
                            act.wait_ge(b_landed[1 - slot],
                                        16 * BATCH * i + (2 * 16 * BATCH - b_elsewhere(1 - slot)))
                            signed(b_rows[:, 1 - slot, :, :], b_raw_at[1 - slot], b_sign).then_inc(
                                b_signed, 1)
                            his, _ = cols_view(down_a_cols[:, slot, :, :].rearrange("p a c -> p (a c)"))
                            hi(his, down_a_raw[:, :, ft_at, :].rearrange("p b f r -> p b (f r)").unsqueeze(
                                3).broadcast_to([P, BATCH, RANK, 3])).then_inc(down_a_hi, 1)
                        act.wait_ge(product_done, step + 1)
                        hi(act_at(h), silu_out[:, half_of(h)]).then_inc(act_hi, 1)
            weights_hi(0, 16 * (FT + 1) // 2)
            act.wait_ge(low_done, LOW_DOWN)
            down_t = t_rows[:, 0:PAIRS * PT].rearrange("p (a t) -> p a t", t=PT)
            for r in range(2):
                at = slice(r * SEQ, (r + 1) * SEQ)
                t_split(r, down_t[:, :, at], banks[:, 4:8, at], t_sign_half).then_inc(t_half_signed, 1)

            def down_chunk_hi(c):
                act.wait_ge(down_chunk_used, c - 1)
                n = FT + c
                slot = n % 2
                act.wait_ge(w_landed[slot], 16 * ((n + 1) // 2))
                m = min(PER_CHUNK, DOWN_TILES - c * PER_CHUNK) * P
                hi(w_hl[:, slot, 0, 0:m], w_raw[:, slot, 0:m]).then_inc(w_hi, 1)

            def x_hi_part(base, ht, h):
                act.wait_ge(x_summed, count(base, ht, h))
                dst = x3_hl if base == L2 else x_hl
                hi(dst[:, 0, ht, half_of(h)], x_res[:, ht, half_of(h)]).then_inc(x_hi, 1)

            def cols_hi(cols, raw):
                his, _ = cols_view(cols)
                return hi(his, raw.unsqueeze(3).broadcast_to([P, BATCH, RANK, 3]))

            def rows_signed(name, rows, raw, gathers):
                act.wait_ge(late_landed[name], 16 * gathers)
                signed(rows, raw, b_sign).then_inc(late_hi, 1)

            def matrix_hi(name, dst, raw):
                act.wait_ge(late_landed[name], 16)
                hi(dst[:, :, 0, :], raw).then_inc(late_hi, 1)

            def low_signed(event, h):
                act.wait_ge(low_done, event)
                dst = t_rows[:, PAIRS * PT + h * HALF:PAIRS * PT + (h + 1) * HALF].rearrange(
                    "p (a t) -> p a t", t=PT)
                src = banks[:, LOW_BANK, :].rearrange("p (a t) -> p a t", t=PT)
                for r in range(2):
                    at = slice(r * SEQ, (r + 1) * SEQ)
                    t_split(r, dst[:, :, at], src[:, :, at], t_sign).then_inc(t_half_signed, 1)

            def l2_low_hi(event, h):
                act.wait_ge(low_done, event)
                for q in (0, 1, 3):
                    for blk in range(2):
                        src = 32 * blk + (64 if q == 3 else 0)
                        last = nc.scalar.activation(l2_t(q, h, blk), l2_low(src, blk), ACT.Copy,
                                                    scale=L2_SCALE)
                last.then_inc(t_half_signed, 2)

            down_chunk_hi(2)
            b_block_signed(0, 16 * BATCH * (B_BLOCKS // 2 + 1))
            for h in range(2):
                x_hi_part(DOWN, 0, h)
            down_chunk_hi(3)
            for h in range(2):
                x_hi_part(DOWN, 1, h)
            down_chunk_hi(4)
            down_chunk_hi(5)
            for h in range(2):
                x_hi_part(DOWN, 2, h)
            act.wait_ge(late_landed["l1_b"], 16 * BATCH)
            for k in range(KT):
                if k == 2:
                    act.wait_ge(act_tile_used, 1)
                last = cols_hi(l1_b_cols[k], l1_b_raw[:, :, k, :])
            last.then_inc(late_hi, 1)
            act.wait_ge(act_tile_used, 3)
            rows_signed("l1_a", l1_a_rows, l1_a_raw, BATCH)
            act.wait_ge(act_tile_used, 7)
            matrix_hi("l2_w", l2_w_hl, l2_w_raw)
            x_hi_part(DOWN, 3, 0)
            act.wait_ge(late_landed["l2_a"], 16 * BATCH)
            act.wait_ge(act_tile_used, FT + 4)
            hi(l2_a_cols[:, :, :, 0:64], l2_a_raw).then_inc(late_hi, 1)
            low_signed(LOW_L1[0], 0)
            act.wait_ge(act_tile_used, FT + 5)
            act.wait_ge(late_landed["l2_b"], 16)
            signed(l2_b_rows, l2_b_raw, sign_col[:, 2:3]).then_inc(late_hi, 1)
            for ht in range(KT):
                x_hi_part(L1, ht, 0)
            x_hi_part(DOWN, 3, 1)
            l2_low_hi(LOW_L2[0], 0)
            low_signed(LOW_L1[1], 1)
            act.wait_ge(late_landed["l3_w"], 16)
            for ht in range(KT):
                x_hi_part(L1, ht, 1)
                hi(l3_w_hl[:, ht, 0, :], l3_w_raw[:, ht, :]).then_inc(late_hi, 1)
            act.wait_ge(late_landed["l3_a"], 16 * BATCH)
            act.wait_ge(late_landed["l3_b"], 16 * BATCH)
            for ht in range(KT):
                x_hi_part(L2, ht, 0)
                if ht == 1:
                    l2_low_hi(LOW_L2[1], 1)
                cols_hi(l3_a_cols[ht], l3_a_raw[:, :, ht, :]).then_inc(late_hi, 1)
            act.wait_ge(group_done, count(L1, KT - 1, 1))
            for ht in range(KT):
                signed(l3_b_rows[:, ht, :], l3_b_raw[:, ht, :], b_sign).then_inc(late_hi, 1)
                if ht == KT - 1:
                    low_signed(LOW_L3[0], 0)
                x_hi_part(L2, ht, 1)
            low_signed(LOW_L3[1], 1)

        @block.vector
        def _(dve):
            def lo(dst, src, hi_part):
                return nc.vector.tensor_tensor(dst, src, hi_part.bitcast(F32), ALU.subtract)

            def add_signed(rows, raw):
                return nc.vector.tensor_tensor(rows, raw, rows.bitcast(F32), ALU.add)

            def cols_lo(cols, raw):
                his, los = cols_view(cols)
                return lo(los, raw, his[:, :, :, 0])

            nc.vector.memset(scratch[:, :], 0.0).then_inc(scratch_zeroed, 1)
            nc.vector.memset(zeros[:, :].bitcast(F32), 0.0).then_inc(zeros_set, 1)
            nc.vector.memset(t_rows[:, :].bitcast(F32), 0.0).then_inc(t_zeroed, 1)
            for c in range(2 * KT):
                h, k = divmod(c, KT)
                if c == PIECES_BEFORE_A:
                    dve.wait_ge(signs_landed, 16)
                    nc.vector.tensor_scalar(t_sign_half[:, :], t_sign, L0_SCALE, None, ALU.mult).then_inc(
                        sign_scaled, 1)
                    for n in range(2 * KT):
                        dve.wait_ge(gu_a_hi, n + 1)
                        cols_lo(gu_a_cols[:, n // KT, n % KT, :],
                                gu_a_raw[:, :, n // KT, n % KT, :]).then_inc(gu_a_ready, 1)
                if h == 0:
                    dve.wait_ge(w_piece_hi, c + 1)
                    at = slice(k * 256, (k + 1) * 256)
                    lo(w_hl[:, 0, 1, at], w_raw[:, 0, at], w_hl[:, 0, 0, at]).then_inc(w_piece_ready, 1)
                dve.wait_ge(x_piece_hi, c + 1)
                lo(x_hl[:, 1, k, half_of(h)], x_res[:, k, half_of(h)], x_hl[:, 0, k, half_of(h)]).then_inc(
                    piece_ready, 1)

            def b_block_add(n, slot):
                dve.wait_ge(b_signed, n + 1)
                add_signed(b_rows[:, slot, :, :], b_raw_at[slot]).then_inc(b_ready, 1)

            def t_add(rows, dst, src, scale):
                return nc.vector.scalar_tensor_tensor(out=dst[rows], in0=src[rows], scalar=scale,
                                                      in1=dst[rows].bitcast(F32), op0=ALU.mult,
                                                      op1=ALU.add)

            def weights_lo(slot, count, m=CHUNK):
                dve.wait_ge(w_hi, count)
                lo(w_hl[:, slot, 1, 0:m], w_raw[:, slot, 0:m], w_hl[:, slot, 0, 0:m]).then_inc(w_ready, 1)

            b_block_add(0, 0)
            weights_lo(1, 1)
            for pair in range(PAIRS):
                gu_low, gu_t = gate_up_values(pair)
                for r in range(2):
                    at = slice(r * SEQ, (r + 1) * SEQ)
                    dve.wait_ge(t_half_signed, 2 * pair + r + 1)
                    last = t_add(slice(64 * r, 64 * r + 64), gu_t[:, :, at], gu_low[:, :, at], L0_SCALE)
                last.then_inc(t_ready, 1)

            def product(h, step):
                dve.wait_ge(silu_done, step + 1)
                nc.vector.tensor_tensor(silu_out[:, half_of(h)], banks[:, 2 * h + 1, :],
                                        silu_out[:, half_of(h)], ALU.mult).then_inc(product_done, 1)

            for h in range(2):
                product(h, h)
                if h == 1:
                    b_block_add(1, 1)
                    dve.wait_ge(down_a_hi, 1)
                    cols_lo(down_a_cols[:, 0, :, :].rearrange("p a c -> p (a c)"),
                            down_a_raw[:, :, 0, :]).then_inc(down_a_ready, 1)
                dve.wait_ge(act_hi, h + 1)
                lo(act_hl[:, 0, 1, half_of(h)], silu_out[:, half_of(h)],
                   act_hl[:, 0, 0, half_of(h)]).then_inc(act_ready, 1)
            with nc.Fori(0, (FT - 1) // 2, engines=[DVE_ENGINE]) as i:
                for u in range(2):
                    ft, slot = 2 * i + (1 + u), (1 + u) % 2
                    ft_at = bass.ds(ft, 1)
                    for h in range(2):
                        step = 4 * i + (2 + 2 * u + h)
                        dve.wait_ge(silu_done, step + 1)
                        nc.vector.tensor_tensor(silu_out[:, half_of(h)], banks[:, 2 * h + 1, :],
                                                silu_out[:, half_of(h)], ALU.mult).then_inc(
                                                    product_done, 1)
                        if h == 0:
                            dve.wait_ge(w_hi, ft + 1)
                            lo(w_hl[:, 1 - slot, 1, :], w_raw[:, 1 - slot, :],
                               w_hl[:, 1 - slot, 0, :]).then_inc(w_ready, 1)
                        else:
                            dve.wait_ge(b_signed, ft + 2)
                            add_signed(b_rows[:, 1 - slot, :, :], b_raw_at[1 - slot]).then_inc(b_ready, 1)
                            dve.wait_ge(down_a_hi, ft + 1)
                            cols_lo(down_a_cols[:, slot, :, :].rearrange("p a c -> p (a c)"),
                                    down_a_raw[:, :, ft_at, :].rearrange(
                                        "p b f r -> p b (f r)")).then_inc(down_a_ready, 1)
                        dve.wait_ge(act_hi, step + 1)
                        lo(act_hl[:, ft_at, 1, half_of(h)].rearrange("p a t -> p (a t)"),
                           silu_out[:, half_of(h)],
                           act_hl[:, ft_at, 0, half_of(h)].rearrange("p a t -> p (a t)")).then_inc(
                               act_ready, 1)
            weights_lo(0, FT + 1)
            down_t = t_rows[:, 0:PAIRS * PT].rearrange("p (a t) -> p a t", t=PT)
            for r in range(2):
                at = slice(r * SEQ, (r + 1) * SEQ)
                dve.wait_ge(t_half_signed, 2 * (LOW_DOWN - 1) + r + 1)
                last = t_add(slice(64 * r, 64 * r + 64), down_t[:, :, at], banks[:, 4:8, at], L0_SCALE)
            last.then_inc(t_ready, 1)

            def down_chunk_lo(c):
                weights_lo((FT + c) % 2, FT + c, min(PER_CHUNK, DOWN_TILES - c * PER_CHUNK) * P)

            def x_sum(base, ht, h):
                dve.wait_ge(group_done, count(base, ht, h))
                nc.vector.tensor_tensor(x_res[:, ht, half_of(h)], bank(base, ht, h),
                                        x_res[:, ht, half_of(h)], ALU.add).then_inc(x_summed, 1)

            def x_lo_part(base, ht, h):
                dve.wait_ge(x_hi, count(base, ht, h))
                dst = x3_hl if base == L2 else x_hl
                lo(dst[:, 1, ht, half_of(h)], x_res[:, ht, half_of(h)],
                   dst[:, 0, ht, half_of(h)]).then_inc(x_ready, 1)

            def late(name):
                dve.wait_ge(late_hi, LATE[name])

            def x_groups(base, which):
                for i, (ht, h) in enumerate(which):
                    x_sum(base, ht, h)
                    if i:
                        x_lo_part(base, *which[i - 1])
                x_lo_part(base, *which[-1])

            down_chunk_lo(2)
            b_block_add(B_BLOCKS - 1, 0)
            x_groups(DOWN, [(0, 0), (0, 1)])
            down_chunk_lo(3)
            x_groups(DOWN, [(1, 0), (1, 1)])
            down_chunk_lo(4)
            down_chunk_lo(5)
            x_groups(DOWN, [(2, 0), (2, 1)])
            late("l1_b")
            for k in range(KT):
                last = cols_lo(l1_b_cols[k], l1_b_raw[:, :, k, :])
            last.then_inc(late_ready, 1)
            late("l1_a")
            add_signed(l1_a_rows, l1_a_raw).then_inc(late_ready, 1)
            x_sum(DOWN, KT - 1, 0)
            late("l2_w")
            for k in range(KT):
                if k == 1:
                    x_lo_part(DOWN, KT - 1, 0)
                last = lo(l2_w_hl[:, k, 1, :], l2_w_raw[:, k, :], l2_w_hl[:, k, 0, :])
            last.then_inc(late_ready, 1)
            late("l2_a")
            lo(l2_a_cols[:, :, :, 64:128], l2_a_raw, l2_a_cols[:, :, :, 0:64]).then_inc(late_ready, 1)

            def low_add(event, h):
                dst = t_rows[:, PAIRS * PT + h * HALF:PAIRS * PT + (h + 1) * HALF].rearrange(
                    "p (a t) -> p a t", t=PT)
                src = banks[:, LOW_BANK, :].rearrange("p (a t) -> p a t", t=PT)
                for r in range(2):
                    at = slice(r * SEQ, (r + 1) * SEQ)
                    dve.wait_ge(t_half_signed, 2 * (event - 1) + r + 1)
                    last = t_add(slice(64 * r, 64 * r + 64), dst[:, :, at], src[:, :, at], 1.0)
                last.then_inc(t_ready, 1)

            def l2_low_lo(event, h):
                dve.wait_ge(t_half_signed, 2 * event)
                for blk in range(2):
                    last = nc.vector.scalar_tensor_tensor(
                        out=l2_t(2, h, blk), in0=l2_low(32 * blk, blk), scalar=L2_SCALE,
                        in1=l2_t(blk, h, blk).bitcast(F32), op0=ALU.mult, op1=ALU.subtract)
                last.then_inc(t_ready, 1)

            low_add(LOW_L1[0], 0)
            late("l2_b")
            add_signed(l2_b_rows, l2_b_raw).then_inc(late_ready, 1)
            x_groups(L1, [(ht, 0) for ht in range(KT)])
            x_groups(DOWN, [(3, 1)])
            l2_low_lo(LOW_L2[0], 0)
            low_add(LOW_L1[1], 1)
            x_groups(L1, [(ht, 1) for ht in range(KT)])
            for ht in range(KT):
                x_sum(L2, ht, 0)
                dve.wait_ge(late_hi, LATE["l2_b"] + 1 + ht)
                lo(l3_w_hl[:, ht, 1, :], l3_w_raw[:, ht, :], l3_w_hl[:, ht, 0, :]).then_inc(late_ready, 1)
                x_lo_part(L2, ht, 0)
                if ht == 1:
                    l2_low_lo(LOW_L2[1], 1)
            for k in range(KT):
                dve.wait_ge(late_hi, LATE["l3_w"] + 1 + k)
                cols_lo(l3_a_cols[k], l3_a_raw[:, :, k, :]).then_inc(late_ready, 1)
            for ht in range(KT):
                x_sum(L2, ht, 1)
                dve.wait_ge(late_hi, LATE["l3_a"] + 1 + ht)
                add_signed(l3_b_rows[:, ht, :], l3_b_raw[:, ht, :]).then_inc(late_ready, 1)
                if ht == KT - 1:
                    low_add(LOW_L3[0], 0)
                x_lo_part(L2, ht, 1)
            dve.wait_ge(bias_landed, 16)
            for n, (ht, tokens) in enumerate(OUT_PARTS):
                h = tokens.start // HALF
                if (ht, h) == (2, 0):
                    low_add(LOW_L3[1], 1)
                dve.wait_ge(group_done, FIRST_OUT + n)
                nc.vector.scalar_tensor_tensor(
                    out=x_res[:, ht, tokens], in0=out_bank(ht, tokens)[:, 0:tokens.stop - tokens.start],
                    scalar=bias_col[:, ht:ht + 1], in1=x_res[:, ht, tokens],
                    op0=ALU.add, op1=ALU.add).then_inc(x_summed, 1)

        @block.tensor
        def _(pe):
            def passes(dst, w_hi_tile, w_lo_tile, m_hi, m_lo, start, stop=False):
                nc.tensor.matmul(dst, w_hi_tile, m_hi, start=start, stop=False)
                nc.tensor.matmul(dst, w_hi_tile, m_lo, start=False, stop=False)
                return nc.tensor.matmul(dst, w_lo_tile, m_hi, start=False, stop=stop)

            def x_tile(k, h, s, x=x_hl):
                return x[:, s, k, half_of(h)]

            def gate_up_k(slot, k, h):
                for w in range(2):
                    at = slice((2 * k + w) * P, (2 * k + w + 1) * P)
                    passes(banks[:, 2 * h + w, :], w_hl[:, slot, 0, at], w_hl[:, slot, 1, at],
                           x_tile(k, h, 0), x_tile(k, h, 1), k == 0, k == KT - 1)

            def gate_up_piece(c):
                h, k = divmod(c, KT)

                def product(w_part, x_part, **flags):
                    for w in range(2):
                        at = slice((2 * k + w) * P, (2 * k + w + 1) * P)
                        nc.tensor.matmul(banks[:, 2 * h + w, :], w_hl[:, 0, w_part, at],
                                         x_tile(k, h, x_part), **flags)

                pe.wait_ge(x_piece_hi, c + 1)
                product(0, 0, start=(k == 0), stop=False)
                if h == 0:
                    pe.wait_ge(w_piece_ready, k + 1)
                product(1, 0, start=False, stop=False)
                pe.wait_ge(piece_ready, c + 1)
                product(0, 1, start=False, stop=(k == KT - 1))

            def gate_up_low(slot, h):
                for w in range(2):
                    for pair in range(2 * h, 2 * h + 2):
                        c0 = (pair % 2) * PT
                        last = nc.tensor.matmul(banks[:, 2 * h + w, c0:c0 + PT],
                                                b_rows[:, slot, pair, w * P:(w + 1) * P],
                                                t_rows[:, (2 * pair + w) * PT:(2 * pair + w + 1) * PT],
                                                start=False, stop=True, skip_group_check=True)
                last.then_inc(gate_up_done, 1)

            def down_low(act_of, slot):
                for pair in range(PAIRS):
                    for s in range(2):
                        last = nc.tensor.matmul(banks[:, 4 + pair, 0:PT], down_a_cols[:, slot, pair, :],
                                                act_of(s, pair), start=False, stop=True,
                                                skip_group_check=True)
                return last

            def gu_low_cols(h):
                pairs = range(2 * h, 2 * h + 2)
                for n in range(2 * KT):
                    w, k = divmod(n, KT)
                    if h == 0:
                        pe.wait_ge(gu_a_ready, n + 1)
                    for pair in pairs:
                        for part in range(2):
                            last = nc.tensor.matmul(
                                banks[:, 4 + pair, w * PT:(w + 1) * PT],
                                gu_a_cols[:, w, k, pair * P:(pair + 1) * P],
                                x_hl[:, part, k, pair_of(pair)], start=(k == 0 and part == 0),
                                stop=(k == KT - 1 and part == 1))
                        if n == 2 * KT - 1:
                            last.then_inc(low_done, 1)

            pe.wait_ge(zeros_set, 1)
            for _ in range(15):
                nc.tensor.matmul(banks[:, 7, 0:PT], zeros[:, 0:P], zeros[:, :], start=True, stop=True)
            for c in range(PIECES_BEFORE_A):
                gate_up_piece(c)
            gu_low_cols(0)
            for c in range(PIECES_BEFORE_A, 2 * KT - 1):
                gate_up_piece(c)
            pe.wait_ge(piece_ready, 2 * KT)
            gu_low_cols(1)
            pe.wait_ge(t_ready, LOW_GATE_UP[PAIRS // 2 - 1])
            pe.wait_ge(b_ready, 1)
            gate_up_low(0, 0)
            gate_up_piece(2 * KT - 1)
            pe.wait_ge(t_ready, LOW_GATE_UP[-1])
            gate_up_low(0, 1)
            for pair in range(PAIRS):
                nc.tensor.matmul(banks[:, 4 + pair, 0:RANK], zeros[:, 0:P], zeros[:, 0:RANK], start=True,
                                 stop=True)

            with nc.Fori(0, (FT - 1) // 2, engines=[PE_ENGINE]) as i:
                for u in range(2):
                    ft, slot = 2 * i + (1 + u), (1 + u) % 2
                    pe.wait_ge(w_ready, ft)
                    for h in range(2):
                        pe.wait_ge(product_done, 2 * ft + (h - 1))
                        for k in range(KT):
                            gate_up_k(slot, k, h)
                        if h == 0:
                            pe.wait_ge(b_ready, ft + 1)
                        gate_up_low(slot, h)
                        if h == 0:
                            pe.wait_ge(down_a_ready, ft)
                            pe.wait_ge(act_ready, 2 * ft)
                            prev = bass.ds(ft - 1, 1)
                            down_low(lambda s, pair: act_hl[:, prev, s, pair_of(pair)].rearrange(
                                "p a t -> p (a t)"), 1 - slot)

            def down_tile(t, halves, freed=None):
                ht, k = divmod(t, FT)
                c, at = divmod(t, PER_CHUNK)
                slot = (FT + c) % 2
                cols = slice(at * P, (at + 1) * P)
                if at == 0:
                    pe.wait_ge(w_ready, FT + c)
                for h in halves:
                    if k == 0 and ht < 2:
                        pe.wait_ge(product_done, 2 * FT - 1 + ht)
                    elif k == 0 and bank_free(DOWN, ht, h):
                        pe.wait_ge(x_summed, bank_free(DOWN, ht, h))
                    last = passes(bank(DOWN, ht, h), w_hl[:, slot, 0, cols], w_hl[:, slot, 1, cols],
                                  act_hl[:, k, 0, half_of(h)], act_hl[:, k, 1, half_of(h)], k == 0,
                                  k == FT - 1)
                if freed is not None:
                    last.then_inc(freed, 1)

            def low_rows(base, ht, h, rows_of, t_base):
                for pair in range(2 * h, 2 * h + 2):
                    c0 = (pair % 2) * PT
                    last = nc.tensor.matmul(bank(base, ht, h)[:, c0:c0 + PT], rows_of(pair),
                                            t_rows[:, t_base + pair * PT:t_base + (pair + 1) * PT],
                                            start=(base == L1 and pair % 2 == 0), stop=True,
                                            skip_group_check=True)
                last.then_inc(group_done, 1)

            def down_rows(ht, h):
                low_rows(DOWN, ht, h, lambda pair: b_rows[
                    :, (FT + ht // 2) % 2, pair, (ht % 2) * P:(ht % 2 + 1) * P], 0)

            for ht in range(KT - 1):
                for k in range(FT):
                    t = ht * FT + k
                    if t == 3:
                        pe.wait_ge(act_ready, 2 * FT)
                        pe.wait_ge(down_a_ready, FT)
                        down_low(lambda s, pair: act_hl[:, FT - 1, s, pair_of(pair)],
                                 (FT - 1) % 2).then_inc(low_done, 1)
                    down_tile(t, range(2), down_chunk_used if t % PER_CHUNK == PER_CHUNK - 1 else None)
                if ht == 0:
                    pe.wait_ge(t_ready, LOW_DOWN)
                    pe.wait_ge(b_ready, FT + 1)
                elif ht == 2:
                    pe.wait_ge(b_ready, B_BLOCKS)
                for h in range(2):
                    down_rows(ht, h)

            def low_cols(cols, h, x):
                for pair in range(2 * h, 2 * h + 2):
                    c0 = (pair % 2) * PT
                    for k in range(KT):
                        for s in range(2):
                            last = nc.tensor.matmul(banks[:, LOW_BANK, c0:c0 + PT],
                                                    cols[k][:, pair * P:(pair + 1) * P],
                                                    x[:, s, k, pair_of(pair)],
                                                    start=(k == 0 and s == 0),
                                                    stop=(k == KT - 1 and s == 1))
                last.then_inc(low_done, 1)

            def l1_groups(h):
                pe.wait_ge(t_ready, LOW_L1[h])
                for ht in range(KT):
                    pe.wait_ge(x_summed, bank_free(L1, ht, h))
                    low_rows(L1, ht, h, lambda pair: l1_a_rows[:, pair, ht * P:(ht + 1) * P], PAIRS * PT)

            for k in range(FT):
                down_tile((KT - 1) * FT + k, [0], act_tile_used)
            down_rows(KT - 1, 0)
            for k in range(FT):
                if k == 4:
                    pe.wait_ge(late_ready, LATE["l1_b"])
                    pe.wait_ge(x_ready, count(DOWN, KT - 1, 0))
                    low_cols(l1_b_cols, 0, x_hl)
                if k == 7:
                    pe.wait_ge(late_ready, LATE["l1_a"])
                    l1_groups(0)
                down_tile((KT - 1) * FT + k, [1], act_tile_used)
            down_rows(KT - 1, 1)

            def main(base, ht, h, w, x, tiles=range(KT)):
                cols = slice(ht * P, (ht + 1) * P)
                if tiles[0] == 0 and bank_free(base, ht, h):
                    pe.wait_ge(x_summed, bank_free(base, ht, h))
                for k in tiles:
                    passes(bank(base, ht, h), w[:, k, 0, cols], w[:, k, 1, cols],
                           x_tile(k, h, 0, x), x_tile(k, h, 1, x), k == 0, k == KT - 1)

            def l2_low_cols(h, tiles=range(KT)):
                for k in tiles:
                    pe.wait_ge(x_ready, count(L1, k, h))
                    for pair in range(2 * h, 2 * h + 2):
                        for s in range(2):
                            last = nc.tensor.matmul(
                                banks[:, L2_LOW_BANK, (pair % 2) * PT:(pair % 2 + 1) * PT],
                                l2_a_cols[:, k, pair, :], x_hl[:, s, k, pair_of(pair)],
                                start=(k == 0 and pair % 2 == 0 and s == 0), stop=True,
                                skip_group_check=True)
                if k == KT - 1:
                    last.then_inc(low_done, 1)

            def l2_main(ht, h, tiles=range(KT)):
                main(L2, ht, h, l2_w_hl, x_hl, tiles)

            def l2_rows(ht, h):
                pe.wait_ge(t_ready, LOW_L2[h])
                nc.tensor.matmul(bank(L2, ht, h), l2_b_rows[:, ht * P:(ht + 1) * P],
                                 t_rows[:, half_of(h)], start=False, stop=True,
                                 skip_group_check=True).then_inc(group_done, 1)

            def l3_group(ht, h):
                main(L3, ht, h, l3_w_hl, x3_hl)
                pe.wait_ge(late_ready, LATE["l3_b"])
                pe.wait_ge(t_ready, LOW_L3[h])
                low_rows(L3, ht, h, lambda pair: l3_b_rows[:, pair, ht * P:(ht + 1) * P], PAIRS * PT)

            pe.wait_ge(late_ready, LATE["l2_a"])
            for k in range(KT):
                l2_low_cols(0, [k])
                l2_main(0, 0, [k])
                if k == 0:
                    l2_main(1, 0, [k])
            pe.wait_ge(x_ready, count(DOWN, KT - 1, 1))
            low_cols(l1_b_cols, 1, x_hl)
            l2_main(1, 0, range(1, KT))
            l1_groups(1)
            pe.wait_ge(late_ready, LATE["l2_b"])
            l2_rows(0, 0)
            l2_rows(1, 0)
            l2_main(2, 0)
            l2_rows(2, 0)
            l2_main(3, 0)
            l2_low_cols(1)
            l2_rows(3, 0)
            l2_main(0, 1)
            l2_main(1, 1)
            l2_rows(0, 1)
            l2_rows(1, 1)
            l2_main(2, 1)
            l2_rows(2, 1)
            l2_main(KT - 1, 1)
            l2_rows(KT - 1, 1)
            pe.wait_ge(late_ready, LATE["l3_a"])
            pe.wait_ge(x_ready, count(L2, KT - 1, 0))
            low_cols(l3_a_cols, 0, x3_hl)
            for ht in range(KT):
                l3_group(ht, 0)
                if ht == 1:
                    pe.wait_ge(x_ready, count(L2, KT - 1, 1))
                    low_cols(l3_a_cols, 1, x3_hl)
            for ht in range(KT - 1):
                l3_group(ht, 1)
            cols = slice((KT - 1) * P, KT * P)
            pe.wait_ge(x_summed, bank_free(L3, KT - 1, 1))
            for pair in (PAIRS - 2, PAIRS - 1):
                dst = out_bank(KT - 1, pair_of(pair))[:, 0:PT]
                for k in range(KT):
                    passes(dst, l3_w_hl[:, k, 0, cols], l3_w_hl[:, k, 1, cols],
                           x3_hl[:, 0, k, pair_of(pair)], x3_hl[:, 1, k, pair_of(pair)], k == 0)
                nc.tensor.matmul(dst, l3_b_rows[:, pair, cols],
                                 t_rows[:, (PAIRS + pair) * PT:(PAIRS + pair + 1) * PT],
                                 start=False, stop=True).then_inc(group_done, 1)


def kernel(**inputs):
    import numpy as np
    import concourse.bacc as bacc
    from concourse.bass_utils import run_bass_kernel_spmd

    a = {k: np.asarray(v) for k, v in inputs.items()}

    def pad_f(m, axis):
        widths = [(0, 0)] * m.ndim
        widths[axis] = (0, FPAD - FFN)
        return np.pad(m, widths)

    def cols_table(t):
        n, r, f = t.shape
        return t.reshape(n, r, f // P, P).transpose(0, 3, 2, 1)

    def gate_up_tiles(w):
        return pad_f(w, 0).reshape(FT, P, KT, P).transpose(0, 3, 2, 1)

    gu = np.stack([gate_up_tiles(a["L0_cond_W_gate"]), gate_up_tiles(a["L0_cond_W_up"])], 3)
    gu = gu.reshape(FT, P, CHUNK)
    down = pad_f(a["L0_cond_W_down"], 1).reshape(KT, P, FT, P).transpose(0, 2, 3, 1)
    down = np.pad(down.reshape(DOWN_TILES, P, P),
                  [(0, DOWN_CHUNKS * PER_CHUNK - DOWN_TILES), (0, 0), (0, 0)])
    down = down.reshape(DOWN_CHUNKS, PER_CHUNK, P, P).transpose(0, 2, 1, 3).reshape(DOWN_CHUNKS, P, CHUNK)

    def rows_ffn(t):
        return pad_f(t[0], 1).reshape(-1, FT, P, RANK).transpose(0, 1, 3, 2)

    up_b = np.stack([rows_ffn(a["L0_cond_B_gate"]), rows_ffn(a["L0_cond_B_up"])], 3)
    up_b = up_b.reshape(-1, FT, RANK, 2 * P)
    down_b = a["L0_cond_B_down"][0].reshape(-1, KT // 2, 2 * P, RANK).transpose(0, 1, 3, 2)

    def square(w):
        return w.T.reshape(KT, P, HID).transpose(1, 0, 2).reshape(P, KT * HID)

    sign = np.zeros((P, 3), np.float32)
    sign[2::4, 0] = -1.0
    sign[1::4, 1] = -1.0
    sign[P // 4:P // 2, 2] = -1.0
    data = {
        "x_t": a["x"].reshape(TOK, HID).T.reshape(KT, P, TOK),
        "weights": np.concatenate([gu, down], 0),
        "indices": np.concatenate([a["itok_B_2_6"], a["itok_B_3_7"], a["itok_B_0_2"],
                                   a["itok_B_6_15"]]).reshape(1, 4 * BATCH),
        "gu_a": np.stack([cols_table(a["L0_cond_A_gate"][0]), cols_table(a["L0_cond_A_up"][0])],
                         2).reshape(ADAPTERS["l0"], P, 2 * KT * RANK),
        "up_b": np.concatenate([up_b, down_b], 1),
        "down_a": cols_table(pad_f(a["L0_cond_A_down"][0], 2)).reshape(ADAPTERS["l0"], P, FT * RANK),
        "l1_b": cols_table(a["L1_cond_B"]).reshape(ADAPTERS["l1"], P, KT * RANK),
        "l1_a": a["L1_cond_A"].transpose(0, 2, 1),
        "l2_w": square(a["L2_cond_W"]),
        "l2_a": cols_table(a["L2_cond_lora_A"].transpose(0, 2, 1)),
        "l2_b": np.tile(a["L2_cond_lora_B_w"].T, (COPIES, 1)),
        "l3_w": square(a["L3_cond_base_weight"]),
        "l3_a": cols_table(a["L3_cond_lora_A_w"]).reshape(ADAPTERS["l3"], P, KT * RANK),
        "l3_b": a["L3_cond_lora_B_w"].transpose(0, 2, 1),
        "bias": a["L3_cond_base_bias"].reshape(KT, P).T,
        "row_signs": sign,
    }
    nc = bacc.Bacc("TRN2", target_bir_lowering=False, num_devices=1)
    arrays, args = {}, []
    for name, v in data.items():
        arrays[name] = np.ascontiguousarray(v)
        args.append(nc.dram_tensor(name, v.shape, mybir.dt.from_np(v.dtype), kind="ExternalInput").ap())
    out_t = nc.dram_tensor("out_t", (KT, P, TOK), F32, kind="ExternalOutput").ap()
    lora_chain_kernel(nc, *args, out_t)
    r = run_bass_kernel_spmd(nc, [arrays], core_ids=[0])
    got = r.results[0]["out_t"]
    return np.ascontiguousarray(got.reshape(HID, TOK).T).reshape(BATCH, SEQ, HID)
```
